# Optimizing a Trainium2 kernel written in Bass

```python
import numpy as np
import jax
import jax.numpy as jnp

def _softmax(x, axis=-1):
    return jax.nn.softmax(x, axis=axis)

def _gelu(x):
    return jax.nn.gelu(x, approximate=True)

def _silu(x):
    return jax.nn.silu(x)

def _sigmoid(x):
    return jax.nn.sigmoid(x)

def _layernorm(x, axis=-1, eps=1e-05):
    m = jnp.mean(x, axis=axis, keepdims=True)
    v = jnp.var(x, axis=axis, keepdims=True)
    return (x - m) / jnp.sqrt(v + eps)

def _scatter_add(tgt, idx, src, axis=0):
    return tgt.at[idx].add(src)

def _segment_sum(src, seg, n):
    return jax.ops.segment_sum(src, seg, n)
kernel_name = 'mk_seq_preln_d1_jaxref_r4_b34938'

def setup_inputs(seed: int=0):
    np.random.seed(seed)
    _w = jnp.asarray

    def _L0_attn_setup():
        import jax, jax.numpy as jnp
        import numpy as np
        HIDDEN = 256
        HEADS = 16
        HEAD_DIM = HIDDEN // HEADS
        SCALE = HEAD_DIM ** (-0.5)
        EPS = 1e-06
        key = jax.random.key(seed)
        k1, k2, k3, k4, k5 = jax.random.split(key, 5)
        B, S = (2, 512)
        std = HIDDEN ** (-0.5)
        return {'x': jax.random.normal(k1, (B, S, HIDDEN), dtype=jnp.float32), 'Wq': jax.random.normal(k2, (HIDDEN, HIDDEN), dtype=jnp.float32) * std, 'Wk': jax.random.normal(k3, (HIDDEN, HIDDEN), dtype=jnp.float32) * std, 'Wv': jax.random.normal(k4, (HIDDEN, HIDDEN), dtype=jnp.float32) * std, 'Wo': jax.random.normal(k5, (HIDDEN, HIDDEN), dtype=jnp.float32) * std}
    _L0_attn_in = _L0_attn_setup()

    def _L0_ffn_setup():
        import jax, jax.numpy as jnp
        import numpy as np
        CAPACITY_RATIO = 0.75
        key = jax.random.key(seed)
        k1, k2, k3 = jax.random.split(key, 3)
        B, L, D = (4, 2048, 256)
        x = jax.random.normal(k1, (B, L, D), dtype=jnp.float32)
        w_router = jax.random.normal(k2, (D,), dtype=jnp.float32) * 0.02
        w_block = jax.random.normal(k3, (D, D), dtype=jnp.float32) * 0.02
        return {'x': x, 'w_router': w_router, 'w_block': w_block}
    _L0_ffn_in = _L0_ffn_setup()
    _d = {'L0_attn_x': _L0_attn_in['x'], 'L0_attn_Wq': _L0_attn_in['Wq'], 'L0_attn_Wk': _L0_attn_in['Wk'], 'L0_attn_Wv': _L0_attn_in['Wv'], 'L0_attn_Wo': _L0_attn_in['Wo'], 'L0_ffn_w_router': _L0_ffn_in['w_router'], 'L0_ffn_w_block': _L0_ffn_in['w_block']}
    _x0 = _d['L0_attn_x']
    _d['L0_attn_x'] = jax.random.normal(jax.random.fold_in(jax.random.key(seed), 1), (8, 512, 256), dtype=_x0.dtype)
    del _x0
    return _d

def reference(L0_attn_x, L0_attn_Wq, L0_attn_Wk, L0_attn_Wv, L0_attn_Wo, L0_ffn_w_router, L0_ffn_w_block):

    def _L0_attn_ref(x, Wq, Wk, Wv, Wo):
        import jax, jax.numpy as jnp
        import numpy as np
        HIDDEN = 256
        HEADS = 16
        HEAD_DIM = HIDDEN // HEADS
        SCALE = HEAD_DIM ** (-0.5)
        EPS = 1e-06
        B, S, H = x.shape

        def proj(W):
            y = jnp.einsum('bsh,oh->bso', x, W)
            return y.reshape(B, S, HEADS, HEAD_DIM).transpose(0, 2, 1, 3)
        q, k, v = (proj(Wq), proj(Wk), proj(Wv))
        scores = jnp.einsum('bhqd,bhkd->bhqk', q, k) * SCALE
        w = jax.nn.sigmoid(scores)
        w = w / (w.sum(axis=-1, keepdims=True) + EPS)
        out = jnp.einsum('bhqk,bhkd->bhqd', w, v)
        out = out.transpose(0, 2, 1, 3).reshape(B, S, H)
        return jnp.einsum('bsh,oh->bso', out, Wo)

    def _L0_ffn_ref(x, w_router, w_block):
        import jax, jax.numpy as jnp
        import numpy as np
        CAPACITY_RATIO = 0.75
        B, L, D = x.shape
        k = max(1, int(L * CAPACITY_RATIO))
        scores = jnp.einsum('bld,d->bl', x, w_router)
        _, top_idx = jax.lax.top_k(scores, k)
        selected = jnp.take_along_axis(x, top_idx[:, :, None], axis=1)
        processed = jax.nn.gelu(jnp.einsum('bkd,de->bke', selected, w_block))
        batch_idx = jnp.arange(B)[:, None]
        out = x.at[batch_idx, top_idx].set(processed)
        return out
    x = L0_attn_x
    x = x + _L0_attn_ref(_layernorm(x, axis=-1), L0_attn_Wq, L0_attn_Wk, L0_attn_Wv, L0_attn_Wo)
    x = x + _L0_ffn_ref(_layernorm(x, axis=-1), L0_ffn_w_router, L0_ffn_w_block)
    return x

_drawn_inputs = setup_inputs


def setup_inputs(seed=0):
    import zlib

    import numpy as np

    out = dict(_drawn_inputs(seed))
    spreads = {}
    factors = {}
    for name, (base, spread) in spreads.items():
        noise = np.random.default_rng([zlib.crc32(name.encode()), seed]).standard_normal(out[name].shape)
        drawn = base * np.exp(spread * noise) if base else spread * noise
        out[name] = jnp.asarray(drawn.astype(out[name].dtype))
    for name, factor in factors.items():
        out[name] = (out[name] * factor).astype(out[name].dtype)
    return out
```

```python
from contextlib import ExitStack

import concourse.bass as bass
from concourse import mybir

F32 = mybir.dt.float32
BF16 = mybir.dt.bfloat16
ALU = mybir.AluOpType
ACT = mybir.ActivationFunctionType
AX_X = mybir.AxisListType.X

P = 128
B, S, H = 8, 512, 256
HEADS = 16
D = H // HEADS
TC = S // P
HC = H // P
SCALE = float(D) ** -0.5
EPS_W = 1e-6
EPS_LN = 1e-5
TOP = int(S * 0.75)
GROUP = 4
GROUPS = HEADS // GROUP
VW = 32
HALF = HEADS // 2
UNITS = HEADS * 2
Q_PART = [0, 1, 2, 0, 1, 0]
K_PART = [0, 0, 0, 1, 1, 2]
SLOTS = len(Q_PART)
ROWS = SLOTS * D
GELU_A = 0.044715
GELU_G = 1.5957691216057308

JOBS = [
    (0, "qk", 2, 0, 0), (2, "qk", 3, 1, 0), (4, "v", 1, 2, 0), (5, "to", 3, 0, -1),
    (7, "at", 0, 1, -1), (8, "at", 1, 2, -1), (10, "y", 0, 0, -1), (11, "y", 1, 1, -1),
    (13, "to", 0, 2, 0), (14, "nt", 0, 0, 1), (15, "nt", 1, 1, 1), (16, "xt", 0, 2, -1),
    (17, "xt", 1, 0, -1), (18, "qk", 0, 1, 1), (19, "sc", 0, 2, -1), (20, "qk", 1, 0, 1),
    (21, "to", 1, 1, 0), (23, "h", 0, 2, -1), (25, "h", 1, 1, -1), (27, "v", 0, 2, 1),
    (29, "to", 2, 1, 0),
]
PER = {"qk": 4, "v": 2, "to": 4, "at": 2, "y": 2, "nt": 2, "xt": 2, "sc": 1, "h": 2}
STEPS = range(-1, B + 1)


def nth(b, per, i=0):
    return b * per + i + 1


def layer(nc, x, wq_t, wk_t, wv_t, wo_t, w_router, w_block, out):
    parts = nc.dram_tensor("qk_parts", (4, 3, P, S), BF16, kind="Internal").ap()
    x_d = x.rearrange("b (s p) h -> b p s h", p=P)
    out_d = out.rearrange("b (s p) h -> b p s h", p=P)

    with ExitStack() as ctx:
        def sb(name, shape, dt=F32):
            return ctx.enter_context(nc.sbuf_tensor(name, shape, dt))

        def sem(name):
            return ctx.enter_context(nc.semaphore(name))

        wq = sb("wq", [P, HC, H])
        wk = sb("wk", [P, HC, H])
        wv = sb("wv", [P, HC, H])
        wo = sb("wo", [P, HC, H])
        wb = sb("wb", [P, HC, H])
        wr_col = sb("wr_col", [P, HC])
        wr = sb("wr", [P, HC, P])
        ident = sb("ident", [P, P])
        before = sb("before", [P, P])
        ones = sb("ones", [P, P])
        minus_half = sb("minus_half", [P, TC])
        x_in = sb("x_in", [P, TC, H])
        xn = sb("xn", [P, TC, H])
        xn_t = sb("xn_t", [P, HC, S])
        stats1 = sb("stats1", [P, TC, 6])
        mv1 = sb("mv1", [P, TC, 5])
        mean1 = sb("mean1", [P, TC])
        ve1 = sb("ve1", [P, TC])
        rstd1 = sb("rstd1", [P, TC])
        split = sb("split", [P, 4, 3, S], BF16)
        rest = sb("rest", [P, 4, S])
        q_st = sb("q_st", [ROWS, HEADS, S], BF16)
        k_st = sb("k_st", [ROWS, HEADS, S], BF16)
        v_x = sb("v_x", [P, TC, HEADS, VW])
        pr = sb("pr", [P, 2, GROUP, 2 * S])
        o_t = sb("o_t", [P, 2, S])
        den = sb("den", [P, GROUPS, TC * GROUP])
        rden = sb("rden", [P, GROUPS, TC * GROUP])
        att = sb("att", [P, TC, H])
        att_t = sb("att_t", [P, HC, S])
        x1 = sb("x1", [P, TC, H])
        xn2 = sb("xn2", [P, TC, H])
        xn2_t = sb("xn2_t", [P, HC, S])
        stats2 = sb("stats2", [P, TC, 6])
        mv2 = sb("mv2", [P, TC, 5])
        mean2 = sb("mean2", [P, TC])
        ve2 = sb("ve2", [P, TC])
        rstd2 = sb("rstd2", [P, TC])
        diagonal = sb("diagonal", [P, S])
        higher = sb("higher", [P, TC, S + P], BF16)
        score = sb("score", [P, TC])
        count = sb("count", [P, TC, 3])
        rank = sb("rank", [P, TC])
        routed = sb("routed", [P, TC])
        passed = sb("passed", [P, TC])
        base = sb("base", [P, TC, H])
        h_sq = sb("h_sq", [P, 2, 2 * H])
        h_arg = sb("h_arg", [P, 2, 2 * H])
        h_sig = sb("h_sig", [P, 2, 2 * H])
        h_out = sb("h_out", [P, TC, H])
        y_out = sb("y_out", [P, TC, H])

        ps_s = ctx.enter_context(nc.psum_tensor("ps_s", [P, 2, 2 * S], F32))
        ps_o = ctx.enter_context(nc.psum_tensor("ps_o", [P, S], F32))
        ps_m = [ctx.enter_context(nc.psum_tensor(f"ps_m{i}", [P, S], F32)) for i in range(3)]

        weights_in = sem("weights_in")
        wo_in = sem("wo_in")
        x_loaded = sem("x_loaded")
        turned = sem("turned")
        spilled = [sem(f"spilled{i}") for i in range(4)]
        stacked = [sem(f"stacked{i}") for i in range(4)]
        zeros_set = sem("zeros_set")
        consts = sem("consts")
        wr_ready = sem("wr_ready")
        ready = {k: sem(f"{k}_ready") for k in PER}
        taken = {k: sem(f"{k}_taken") for k in PER}
        scores_done = sem("scores_done")
        sigmoid_done = sem("sigmoid_done")
        av_done = sem("av_done")
        o_taken = sem("o_taken")
        part1 = sem("part1")
        part2 = sem("part2")
        part3 = sem("part3")
        stats1_done = sem("stats1_done")
        rstd1_done = sem("rstd1_done")
        ln1_done = sem("ln1_done")
        stats2_done = sem("stats2_done")
        rstd2_done = sem("rstd2_done")
        ln2_done = sem("ln2_done")
        den_done = sem("den_done")
        rank_done = sem("rank_done")
        base_done = sem("base_done")
        square_done = sem("square_done")
        arg_done = sem("arg_done")
        gate_done = sem("gate_done")
        out_ready = sem("out_ready")

        def to_view(bank):
            return ps_m[bank][:, :].rearrange("p (m w) -> p m w", w=VW)

        BANK = {(k, i): bank for _, k, i, bank, _ in JOBS}

        def has(step, off):
            return 0 <= step + off < B

        def last_user(step, flags, n):
            bank = JOBS[n][3]
            for m in reversed(range(n)):
                if JOBS[m][3] == bank and flags[JOBS[m][4]]:
                    return JOBS[m], 0
            if isinstance(step, int) and step - 1 < -1:
                return None
            before_flags = {-1: False, 0: False, 1: False}
            for off in (-1, 0, 1):
                before_flags[off] = has(step - 1, off) if isinstance(step, int) else off >= 0
            for m in reversed(range(len(JOBS))):
                if JOBS[m][3] == bank and before_flags[JOBS[m][4]]:
                    return JOBS[m], -1
            return None

        block = ctx.enter_context(nc.Block())

        def run_steps(eng, step):
            def flags(b):
                return {off: has(b, off) for off in (-1, 0, 1)}
            step(-1, flags(-1))
            step(0, flags(0))
            with eng.Fori(1, B - 1) as b:
                step(b, flags(1))
            step(B - 1, flags(B - 1))
            step(B, flags(B))

        @block.sync
        def _(sp):
            def load_x(b):
                sp.dma_start(x_in[:, :, :], x_d[b]).then_inc(x_loaded, 16)

            sp.dma_start(x_in[:, :, :], x_d[0]).then_inc(x_loaded, 16)
            for w, w_d in ((wq, wq_t), (wk, wk_t), (wv, wv_t)):
                sp.dma_start(w[:, :, :], w_d.rearrange("(c p) o -> p c o", p=P)).then_inc(weights_in, 16)
            for w, w_d in ((wo, wo_t), (wb, w_block)):
                sp.dma_start(w[:, :, :], w_d.rearrange("(c p) o -> p c o", p=P)).then_inc(wo_in, 16)
            for c in range(HC):
                sp.dma_start(wr_col[:, c:c + 1],
                             w_router[c * P:(c + 1) * P].rearrange("(p o) -> p o", o=1)).then_inc(wo_in, 16)

            def spill(value, i):
                sp.wait_ge(part3, value["split", i])
                if value["read", i] is not None:
                    sp.wait_ge(stacked[i], value["read", i])
                sp.dma_start(parts[i].rearrange("t p n -> p t n"), split[:, i, :, :]).then_inc(spilled[i], 16)

            def stack(value, i):
                half, dst, order = i // 2, (q_st, k_st)[i % 2], (Q_PART, K_PART)[i % 2]
                sp.wait_ge(spilled[i], value["spilled", i])
                if value["scored", i] is not None:
                    sp.wait_ge(scores_done, value["scored", i])
                for s, part in enumerate(order):
                    sp.dma_start(dst[s * D:(s + 1) * D, half * HALF:(half + 1) * HALF, :],
                                 parts[i, part].rearrange("(h d) n -> d h n", d=D)).then_inc(stacked[i], 16)

            def values(b, on):
                value = {}
                for i, off in ((2, 0), (3, 0), (0, 1), (1, 1)):
                    if not on[off]:
                        continue
                    m = b + off
                    first = isinstance(m, int) and m == 0
                    value["split", i] = nth(m, 4, i)
                    value["read", i] = None if first else m * (16 * SLOTS)
                    value["spilled", i] = m * 16 + 16
                    value["scored", i] = None if first else (m - 1) * UNITS + (i // 2 + 1) * UNITS // 2
                if on[1] and not (isinstance(b, int) and b == -1):
                    value["normed"] = nth(b, 1)
                if on[0] and not (isinstance(b, int) and b == 0):
                    value["based"] = nth(b - 1, 1)
                if on[-1]:
                    value["out"] = nth(b - 1, 1)
                if not isinstance(b, int):
                    value = {k: sp.to_reg(v) if v is not None else None for k, v in value.items()}
                return value

            def step(b, on):
                value = values(b, on)
                if "normed" in value:
                    sp.wait_ge(ln1_done, value["normed"])
                    load_x(b + 1)
                if on[0]:
                    spill(value, 2)
                    spill(value, 3)
                    stack(value, 2)
                    stack(value, 3)
                if on[1]:
                    spill(value, 0)
                    spill(value, 1)
                    stack(value, 0)
                    stack(value, 1)
                if on[0]:
                    if "based" in value:
                        sp.wait_ge(base_done, value["based"])
                    sp.dma_start(x1[:, :, :], x_d[b]).then_inc(turned, 16)
                if on[-1]:
                    sp.wait_ge(out_ready, value["out"])
                    sp.dma_start(out_d[b - 1], y_out[:, :, :]).then_inc(turned, 16)

            run_steps(sp, step)
            sp.wait_ge(turned, 16 * 2 * B)

        @block.tensor
        def _(pe):
            def transposes(bank, src, c):
                for s in range(TC):
                    mm = nc.tensor.transpose(ps_m[bank][:, s * P:(s + 1) * P], src[:, s, c * P:(c + 1) * P],
                                             ident[:, :])
                return mm

            def job(b, n, on):
                _, kind, i, bank, off = JOBS[n]
                if not on[off]:
                    return
                m = b + off
                user = last_user(b, on, n)
                if user is not None:
                    (_, k2, i2, _, off2), back = user
                    pe.wait_ge(taken[k2], nth(b + back + off2, PER[k2], i2))
                ps = ps_m[bank]
                if kind == "nt":
                    pe.wait_ge(ln1_done, nth(m, 1))
                    mm = transposes(bank, xn, i)
                elif kind == "qk":
                    w, half = (wq, wk)[i % 2], i // 2
                    pe.wait_ge(taken["nt"], nth(m, 2, 1))
                    for c in range(HC):
                        mm = nc.tensor.matmul(ps[:, :], w[:, c, half * P:(half + 1) * P], xn_t[:, c, :],
                                              start=c == 0, stop=c == HC - 1)
                elif kind == "v":
                    pe.wait_ge(taken["nt"], nth(m, 2, 1))
                    for s in range(TC):
                        for c in range(HC):
                            mm = nc.tensor.matmul(ps[:, s * P:(s + 1) * P], xn_t[:, c, s * P:(s + 1) * P],
                                                  wv[:, c, i * P:(i + 1) * P], start=c == 0, stop=c == HC - 1)
                elif kind == "to":
                    pe.wait_ge(o_taken, nth(m, GROUPS, i))
                    for s in range(TC):
                        mm = nc.tensor.transpose(ps[:, s * P:(s + 1) * P], o_t[:, i % 2, s * P:(s + 1) * P],
                                                 ident[:, :])
                elif kind == "at":
                    pe.wait_ge(taken["to"], nth(m, GROUPS, GROUPS - 1))
                    mm = transposes(bank, att, i)
                elif kind == "y":
                    pe.wait_ge(taken["at"], nth(m, 2, 1))
                    for s in range(2):
                        t = 2 * i + s
                        for c in range(HC):
                            mm = nc.tensor.matmul(ps[:, s * H:(s + 1) * H], att_t[:, c, t * P:(t + 1) * P],
                                                  wo[:, c, :], start=c == 0, stop=c == HC - 1)
                elif kind == "xt":
                    pe.wait_ge(ln2_done, nth(m, 1))
                    mm = transposes(bank, xn2, i)
                elif kind == "sc":
                    pe.wait_ge(taken["xt"], nth(m, 2, 1))
                    for c in range(HC):
                        mm = nc.tensor.matmul(ps[:, :], wr[:, c, :], xn2_t[:, c, :], start=c == 0, stop=c == HC - 1)
                elif kind == "h":
                    for s in range(2):
                        t = 2 * i + s
                        for c in range(HC):
                            mm = nc.tensor.matmul(ps[:, s * H:(s + 1) * H], xn2_t[:, c, t * P:(t + 1) * P],
                                                  wb[:, c, :], start=c == 0, stop=c == HC - 1)
                mm.then_inc(ready[kind], 1)

            def scores(b, n):
                g, p, j = n // 8, n // 4 % 2, n % 4
                h = GROUP * g + j
                if n % (UNITS // 2) == 0:
                    for i in (2 * (n * 2 // UNITS), 2 * (n * 2 // UNITS) + 1):
                        pe.wait_ge(stacked[i], (b + 1) * (16 * SLOTS))
                if not (isinstance(b, int) and b == 0 and n < 2):
                    pe.wait_ge(sigmoid_done, b * UNITS + n - 1)
                for kk in range(2):
                    kc = 2 * p + kk
                    mm = nc.tensor.matmul(ps_s[:, n % 2, kk * S:(kk + 1) * S], k_st[:, h, kc * P:(kc + 1) * P],
                                          q_st[:, h, :], start=True, stop=True)
                mm.then_inc(scores_done, 1)

            def weighted_sum(b, r, kk):
                g, p = r // 2, r % 2
                kc = 2 * p + kk
                if kk == 0:
                    pe.wait_ge(sigmoid_done, b * UNITS + 4 * r + 4)
                    if p == 0:
                        if g % 2 == 0:
                            pe.wait_ge(taken["v"], nth(b, 2, g // 2))
                        if not (isinstance(b, int) and b == 0 and g == 0):
                            pe.wait_ge(o_taken, b * GROUPS + g)
                for j in range(GROUP):
                    mm = nc.tensor.matmul(ps_o[j * VW:(j + 1) * VW, :], v_x[:, kc, GROUP * g + j, :],
                                          pr[:, p, j, kk * S:(kk + 1) * S], start=kc == 0, stop=kc == TC - 1)
                mm.then_inc(av_done, 1)

            def step(b, on):
                for n in range(UNITS):
                    if on[0]:
                        scores(b, n)
                    if n % 2 == 1:
                        r, kk = n // 4 - 1, n % 4 // 2
                        if r < 0 and on[-1]:
                            weighted_sum(b - 1, r + 2 * GROUPS, kk)
                        if r >= 0 and on[0]:
                            weighted_sum(b, r, kk)
                    for m in range(len(JOBS)):
                        if JOBS[m][0] == n:
                            job(b, m, on)

            pe.wait_ge(consts, 1)
            pe.wait_ge(weights_in, 48)
            pe.wait_ge(wo_in, 16 * (2 + HC))
            pe.wait_ge(wr_ready, HC)
            run_steps(pe, step)

        @block.scalar
        def _(act):
            def copy(kind, b, i, dst):
                act.wait_ge(ready[kind], nth(b, PER[kind], i))
                nc.scalar.copy(dst, ps_m[BANK[kind, i]][:, :]).then_inc(taken[kind], 1)

            def first_part(b, i):
                act.wait_ge(ready["qk"], nth(b, 4, i))
                if not (isinstance(b, int) and b == 0):
                    act.wait_ge(spilled[i], b * 16)
                nc.scalar.copy(split[:, i, 0, :], ps_m[BANK["qk", i]][:, :]).then_inc(part1, 1)

            def values(b, i):
                act.wait_ge(ready["v"], nth(b, 2, i))
                if not (isinstance(b, int) and b == 0):
                    act.wait_ge(av_done, (b - 1) * 4 * GROUPS + (i + 1) * 2 * GROUPS)
                nc.scalar.copy(v_x[:, :, i * HALF:(i + 1) * HALF, 0:D],
                               ps_m[BANK["v", i]][:, :].rearrange("p (t h d) -> p t h d", t=TC, d=D)
                               ).then_inc(taken["v"], 1)

            def take_o(b, g):
                act.wait_ge(av_done, nth(b, 4 * GROUPS, 4 * g + 3))
                if not (isinstance(b, int) and b == 0 and g < 2):
                    act.wait_ge(ready["to"], b * GROUPS + g - 1)
                nc.scalar.copy(o_t[:, g % 2, :], ps_o[:, :]).then_inc(o_taken, 1)

            def sigmoid(b, n):
                r, j = n // 4, n % 4
                act.wait_ge(scores_done, b * UNITS + n + 1)
                if j == 0 and not (isinstance(b, int) and b == 0 and r < 2):
                    act.wait_ge(av_done, b * 4 * GROUPS + 2 * (r - 1))
                nc.scalar.activation(pr[:, r % 2, j, :], ps_s[:, n % 2, :], ACT.Sigmoid,
                                     scale=SCALE).then_inc(sigmoid_done, 1)

            def square(b, i):
                act.wait_ge(ready["h"], nth(b, 2, i))
                nc.scalar.activation(h_sq[:, i, :], ps_m[BANK["h", i]][:, :], ACT.Square).then_inc(square_done, 1)

            def gate(b, i):
                act.wait_ge(arg_done, nth(b, 2, i))
                nc.scalar.activation(h_sig[:, i, :], h_arg[:, i, :], ACT.Sigmoid,
                                     scale=GELU_G * GELU_A).then_inc(gate_done, 1)

            def step(b, on):
                for n in range(UNITS):
                    if on[0]:
                        sigmoid(b, n)
                        if n == 1:
                            first_part(b, 2)
                        if n == 3:
                            first_part(b, 3)
                        if n == 6:
                            values(b, 1)
                        if n == 12:
                            take_o(b, 0)
                        if n == 20:
                            take_o(b, 1)
                        if n == 28:
                            take_o(b, 2)
                    if on[-1]:
                        if n == 4:
                            take_o(b - 1, 3)
                        if n == 8:
                            copy("at", b - 1, 0, att_t[:, 0, :])
                        if n == 9:
                            copy("at", b - 1, 1, att_t[:, 1, :])
                        if n == 17:
                            copy("xt", b - 1, 0, xn2_t[:, 0, :])
                        if n == 18:
                            copy("xt", b - 1, 1, xn2_t[:, 1, :])
                        if n == 24:
                            square(b - 1, 0)
                        if n == 25:
                            gate(b - 1, 0)
                        if n == 26:
                            square(b - 1, 1)
                        if n == 27:
                            gate(b - 1, 1)
                    if on[1]:
                        if n == 15:
                            copy("nt", b + 1, 0, xn_t[:, 0, :])
                        if n == 16:
                            copy("nt", b + 1, 1, xn_t[:, 1, :])
                        if n == 19:
                            first_part(b + 1, 0)
                        if n == 21:
                            first_part(b + 1, 1)
                        if n == 28:
                            values(b + 1, 0)

            act.wait_ge(consts, 1)
            run_steps(act, step)

        @block.vector
        def _(dve):
            def layernorm(b, src, loaded, stats, mv, mean, ve, rstd, stats_done, rstd_done, dst, done, used):
                dve.wait_ge(*loaded)
                for s in range(TC):
                    op = nc.vector.bn_stats(stats[:, s, :], src[:, s, :])
                op.then_inc(stats_done, 1)
                dve.wait_ge(stats_done, nth(b, 4, 0))
                m0, s0, m1, s1 = (stats[:, :, k] for k in (1, 2, 4, 5))
                nc.vector.tensor_tensor(mv[:, :, 0], m0, m1, ALU.add)
                nc.vector.tensor_tensor(mv[:, :, 1], m0, m1, ALU.subtract)
                nc.vector.tensor_tensor(mv[:, :, 2], s0, s1, ALU.add).then_inc(stats_done, 1)
                dve.wait_ge(stats_done, nth(b, 4, 1))
                nc.vector.tensor_scalar(mean[:, :], mv[:, :, 0], 0.5, None, ALU.mult)
                nc.vector.tensor_scalar(mv[:, :, 3], mv[:, :, 2], 1.0 / H, EPS_LN, ALU.mult, ALU.add)
                nc.vector.scalar_tensor_tensor(mv[:, :, 4], mv[:, :, 1], 0.25, mv[:, :, 1],
                                               ALU.mult, ALU.mult).then_inc(stats_done, 1)
                dve.wait_ge(stats_done, nth(b, 4, 2))
                nc.vector.tensor_tensor(ve[:, :], mv[:, :, 3], mv[:, :, 4], ALU.add).then_inc(stats_done, 1)
                dve.wait_ge(rstd_done, nth(b, 1))
                if used is not None:
                    dve.wait_ge(*used)
                for s in range(TC):
                    op = nc.vector.tensor_scalar(dst[:, s, :], src[:, s, :], mean[:, s:s + 1], rstd[:, s:s + 1],
                                                 ALU.subtract, ALU.mult)
                op.then_inc(done, 1)

            def split_rest(b, i):
                dve.wait_ge(part1, nth(b, 4, i))
                if not (isinstance(b, int) and b == 0):
                    dve.wait_ge(part3, nth(b - 1, 4, i))
                nc.vector.tensor_tensor(rest[:, i, :], ps_m[BANK["qk", i]][:, :], split[:, i, 0, :],
                                        ALU.subtract).then_inc(taken["qk"], 1)
                dve.wait_ge(taken["qk"], nth(b, 4, i))
                nc.vector.tensor_copy(split[:, i, 1, :], rest[:, i, :]).then_inc(part2, 1)

            def normalise(b, g):
                view = to_view(BANK["to", g])
                dve.wait_ge(ready["to"], nth(b, GROUPS, g))
                nc.vector.tensor_scalar(den[:, g, :], view[:, :, D], EPS_W, None, ALU.add).then_inc(den_done, 1)
                dve.wait_ge(den_done, nth(b, 2 * GROUPS, 2 * g))
                nc.vector.reciprocal(rden[:, g, :], den[:, g, :]).then_inc(den_done, 1)
                dve.wait_ge(den_done, nth(b, 2 * GROUPS, 2 * g + 1))
                if g == 0 and not (isinstance(b, int) and b == 0):
                    dve.wait_ge(ready["at"], nth(b - 1, 2, 1))
                w = GROUP * D
                nc.vector.tensor_tensor(
                    att[:, :, g * w:(g + 1) * w].rearrange("p t (j d) -> p t j d", d=D),
                    view[:, :, 0:D].rearrange("p (t j) d -> p t j d", t=TC),
                    rden[:, g, :].rearrange("p (t j) -> p t j", t=TC).unsqueeze(3).broadcast_to([P, TC, GROUP, D]),
                    ALU.mult).then_inc(taken["to"], 1)

            def residual(b, i):
                dve.wait_ge(ready["y"], nth(b, 2, i))
                dve.wait_ge(turned, 32 * b + 16)
                nc.vector.tensor_tensor(x1[:, 2 * i:2 * i + 2, :],
                                        ps_m[BANK["y", i]][:, :].rearrange("p (t h) -> p t h", t=2),
                                        x1[:, 2 * i:2 * i + 2, :], ALU.add).then_inc(taken["y"], 1)

            def route(b):
                ps = ps_m[BANK["sc", 0]]
                dve.wait_ge(ready["sc"], nth(b, 1))
                for t in range(TC):
                    op = nc.vector.tensor_tensor_reduce(diagonal[:, t * P:(t + 1) * P], ps[:, t * P:(t + 1) * P],
                                                        ident[:, :], 1.0, 0.0, ALU.mult, ALU.add,
                                                        score[:, t:t + 1])
                op.then_inc(rank_done, 1)
                dve.wait_ge(rank_done, nth(b, 4, 0))
                for t in range(TC):
                    own = score[:, t:t + 1]
                    if t > 0:
                        nc.vector.tensor_scalar(higher[:, t, 0:t * P], ps[:, 0:t * P], own, None, ALU.is_ge, ALU.add,
                                                accum_out=count[:, t, 0:1])
                    nc.vector.tensor_scalar(higher[:, t, t * P:S], ps[:, t * P:S], own, None, ALU.is_gt, ALU.add,
                                            accum_out=count[:, t, 1:2])
                    op = nc.vector.scalar_tensor_tensor(higher[:, t, S:S + P], ps[:, t * P:(t + 1) * P], own,
                                                        before[:, :], ALU.is_equal, ALU.mult,
                                                        accum_out=count[:, t, 2:3])
                op.then_inc(taken["sc"], 1)
                dve.wait_ge(taken["sc"], nth(b, 1))
                nc.vector.tensor_reduce(rank[:, :], count[:, :, :], AX_X, ALU.add).then_inc(rank_done, 1)
                dve.wait_ge(rank_done, nth(b, 4, 1))
                nc.vector.tensor_scalar(routed[:, :], rank[:, :], float(TOP), None, ALU.is_lt).then_inc(rank_done, 1)
                nc.vector.tensor_scalar(passed[:, :], rank[:, :], float(TOP), None, ALU.is_ge).then_inc(rank_done, 1)
                dve.wait_ge(rank_done, nth(b, 4, 3))
                for t in range(TC):
                    op = nc.vector.scalar_tensor_tensor(base[:, t, :], xn2[:, t, :], passed[:, t:t + 1], x1[:, t, :],
                                                        ALU.mult, ALU.add)
                op.then_inc(base_done, 1)

            def gelu_arg(b, i):
                dve.wait_ge(square_done, nth(b, 2, i))
                nc.vector.scalar_tensor_tensor(h_arg[:, i, :], h_sq[:, i, :], 1.0 / GELU_A,
                                               ps_m[BANK["h", i]][:, :], ALU.add, ALU.mult).then_inc(arg_done, 1)

            def gelu(b, i):
                dve.wait_ge(gate_done, nth(b, 2, i))
                for s in range(2):
                    t = 2 * i + s
                    op = nc.vector.scalar_tensor_tensor(h_out[:, t, :], h_sig[:, i, s * H:(s + 1) * H],
                                                        routed[:, t:t + 1],
                                                        ps_m[BANK["h", i]][:, s * H:(s + 1) * H],
                                                        ALU.mult, ALU.mult)
                op.then_inc(taken["h"], 1)

            def step(b, on):
                if on[0]:
                    split_rest(b, 2)
                    split_rest(b, 3)
                if on[-1]:
                    normalise(b - 1, 3)
                if on[1]:
                    used = None if isinstance(b, int) and b == -1 else (ready["nt"], nth(b, 2, 1))
                    layernorm(b + 1, x_in, (x_loaded, 16 * (b + 1) + 16), stats1, mv1, mean1, ve1, rstd1,
                              stats1_done, rstd1_done, xn, ln1_done, used)
                if on[-1]:
                    residual(b - 1, 0)
                    residual(b - 1, 1)
                    layernorm(b - 1, x1, (taken["y"], nth(b - 1, 2, 1)), stats2, mv2, mean2, ve2, rstd2,
                              stats2_done, rstd2_done, xn2, ln2_done, None)
                if on[0]:
                    normalise(b, 0)
                if on[1]:
                    split_rest(b + 1, 0)
                    split_rest(b + 1, 1)
                if on[-1]:
                    route(b - 1)
                if on[0]:
                    normalise(b, 1)
                if on[-1]:
                    gelu_arg(b - 1, 0)
                    gelu(b - 1, 0)
                    gelu_arg(b - 1, 1)
                    gelu(b - 1, 1)
                if on[0]:
                    normalise(b, 2)

            dve.wait_ge(consts, 1)
            dve.wait_ge(wo_in, 16 * (2 + HC))
            for c in range(HC):
                nc.vector.tensor_scalar(wr[:, c, :], ones[:, :], wr_col[:, c:c + 1], None,
                                        ALU.mult).then_inc(wr_ready, 1)
            run_steps(dve, step)

        @block.gpsimd
        def _(pool):
            nc.gpsimd.memset(ident[:, :], 0.0)
            nc.gpsimd.memset(before[:, :], 0.0)
            nc.gpsimd.memset(ones[:, :], 1.0)
            nc.gpsimd.memset(minus_half[:, :], -0.5)
            nc.gpsimd.memset(count[:, :, :], 0.0)
            nc.gpsimd.memset(v_x[:, :, :, :], 1.0).then_inc(zeros_set, 1)
            pool.wait_ge(zeros_set, 1)
            nc.gpsimd.affine_select(out=ident[:, :], in_=ident[:, :], compare_op=ALU.not_equal, fill=1.0,
                                    base=0, pattern=[[-1, P]], channel_multiplier=1)
            nc.gpsimd.affine_select(out=before[:, :], in_=before[:, :], compare_op=ALU.is_ge, fill=1.0,
                                    base=0, pattern=[[1, P]], channel_multiplier=-1).then_inc(consts, 1)

            def third_part(b, i):
                pool.wait_ge(part2, nth(b, 4, i))
                nc.gpsimd.tensor_tensor(split[:, i, 2, :], rest[:, i, :], split[:, i, 1, :],
                                        ALU.subtract).then_inc(part3, 1)

            def inverse_root(b, ve, rstd, stats_done, rstd_done):
                pool.wait_ge(stats_done, nth(b, 4, 3))
                nc.gpsimd.tensor_tensor(rstd[:, :], ve[:, :], minus_half[:, :], ALU.pow).then_inc(rstd_done, 1)

            def output(b):
                pool.wait_ge(taken["h"], nth(b, 2, 1))
                pool.wait_ge(base_done, nth(b, 1))
                pool.wait_ge(turned, 32 * b + 16)
                nc.gpsimd.tensor_tensor(y_out[:, :, :], base[:, :, :], h_out[:, :, :],
                                        ALU.add).then_inc(out_ready, 1)

            def step(b, on):
                if on[0]:
                    third_part(b, 2)
                    third_part(b, 3)
                if on[1]:
                    inverse_root(b + 1, ve1, rstd1, stats1_done, rstd1_done)
                if on[-1]:
                    inverse_root(b - 1, ve2, rstd2, stats2_done, rstd2_done)
                if on[1]:
                    third_part(b + 1, 0)
                    third_part(b + 1, 1)
                if on[-1]:
                    output(b - 1)

            run_steps(pool, step)


def kernel(**inputs):
    import numpy as _np
    import concourse.bacc as _bacc
    from concourse import mybir as _mybir
    from concourse.bass_utils import run_bass_kernel_spmd as _run

    nc = _bacc.Bacc("TRN2", target_bir_lowering=False, num_devices=1)
    arrays, args = {}, []
    for name in ("L0_attn_x", "L0_attn_Wq", "L0_attn_Wk", "L0_attn_Wv", "L0_attn_Wo",
                 "L0_ffn_w_router", "L0_ffn_w_block"):
        a = _np.asarray(inputs[name])
        if name.startswith("L0_attn_W"):
            a = a.T
        a = _np.ascontiguousarray(a)
        arrays[f"in_{name}"] = a
        args.append(nc.dram_tensor(f"in_{name}", a.shape, _mybir.dt.from_np(a.dtype), kind="ExternalInput").ap())
    args.append(nc.dram_tensor("out_0", (B, S, H), F32, kind="ExternalOutput").ap())
    layer(nc, *args)
    r = _run(nc, [arrays], core_ids=[0])
    return r.results[0]["out_0"]
```

```python
from contextlib import ExitStack

import concourse.bass as bass
from concourse import mybir

F32 = mybir.dt.float32
F32R = mybir.dt.float32r
BF16 = mybir.dt.bfloat16
ALU = mybir.AluOpType
ACT = mybir.ActivationFunctionType
AX_X = mybir.AxisListType.X

P = 128
B, S, H = 8, 512, 256
HEADS = 16
D = H // HEADS
TC = S // P
HC = H // P
SCALE = float(D) ** -0.5
EPS_W = 1e-6
EPS_LN = 1e-5
TOP = int(S * 0.75)
GROUP = 4
GROUPS = HEADS // GROUP
VW = 32
HALF = HEADS // 2
UNITS = HEADS * 2
Q_PART = [0, 1, 2, 0, 1, 0]
K_PART = [0, 0, 0, 1, 1, 2]
SLOTS = len(Q_PART)
ROWS = SLOTS * D
GELU_A = 0.044715
GELU_G = 1.5957691216057308

JOBS = [
    (1, "qk", 2, 0, 0), (5, "to", 3, 1, -1), (6, "qk", 3, 2, 0), (8, "at", 0, 0, -1),
    (9, "at", 1, 1, -1), (10, "nt", 0, 2, 1), (11, "nt", 1, 0, 1), (12, "y", 0, 1, -1),
    (13, "y", 1, 2, -1), (14, "to", 0, 0, 0), (15, "qk", 0, 1, 1), (17, "qk", 1, 2, 1),
    (19, "xt", 0, 0, -1), (20, "xt", 1, 1, -1), (21, "sc", 0, 2, -1), (22, "to", 1, 0, 0),
    (24, "h", 0, 1, -1), (26, "h", 1, 2, -1), (28, "v", 0, 0, 1), (29, "v", 1, 1, 1),
    (30, "to", 2, 2, 0),
]
PER = {"qk": 4, "v": 2, "to": 4, "at": 2, "y": 2, "nt": 2, "xt": 2, "sc": 1, "h": 2}
PASSES = ((0, 0), (0, 1), (1, 0))
STEPS = range(-1, B + 1)


def nth(b, per, i=0):
    return b * per + i + 1


def layer(nc, x, wq_t, wk_t, wv_t, wo_t, w_router, w_block, out):
    parts = nc.dram_tensor("qk_parts", (4, 3, P, S), BF16, kind="Internal").ap()
    x_d = x.rearrange("b (s p) h -> b p s h", p=P)
    out_d = out.rearrange("b (s p) h -> b p s h", p=P)

    with ExitStack() as ctx:
        def sb(name, shape, dt=F32):
            return ctx.enter_context(nc.sbuf_tensor(name, shape, dt))

        def sem(name):
            return ctx.enter_context(nc.semaphore(name))

        wq, wk, wv, wo, wb = (sb(name, [P, 2, HC, H], F32R) for name in ("wq", "wk", "wv", "wo", "wb"))
        wr = sb("wr", [P, H])
        ident = sb("ident", [P, P])
        before = sb("before", [P, P])
        minus_half = sb("minus_half", [P, TC])
        x_in = sb("x_in", [P, TC, H])
        xn = sb("xn", [P, TC, H])
        xn_t = sb("xn_t", [P, 2, HC, S], F32R)
        stats1 = sb("stats1", [P, TC, 6])
        mv1 = sb("mv1", [P, TC, 5])
        mean1 = sb("mean1", [P, TC])
        ve1 = sb("ve1", [P, TC])
        rstd1 = sb("rstd1", [P, TC])
        split = sb("split", [P, 4, 3, S], BF16)
        rest = sb("rest", [P, 4, S])
        q_st = sb("q_st", [ROWS, HEADS, S], BF16)
        k_st = sb("k_st", [ROWS, HEADS, S], BF16)
        v_in = sb("v_in", [P, TC, H])
        v_x = sb("v_x", [P, TC, HEADS, VW])
        pr = sb("pr", [P, 2, GROUP, 2 * S])
        o_t = sb("o_t", [P, 2, S])
        den = sb("den", [P, GROUPS, TC * GROUP])
        rden = sb("rden", [P, GROUPS, TC * GROUP])
        att = sb("att", [P, TC, H])
        att_t = sb("att_t", [P, 2, HC, S], F32R)
        x1 = sb("x1", [P, TC, H])
        xn2 = sb("xn2", [P, TC, H])
        xn2_t = sb("xn2_t", [P, 2, HC, S], F32R)
        stats2 = sb("stats2", [P, TC, 6])
        mv2 = sb("mv2", [P, TC, 5])
        mean2 = sb("mean2", [P, TC])
        ve2 = sb("ve2", [P, TC])
        rstd2 = sb("rstd2", [P, TC])
        s_row = sb("s_row", [P, S])
        product = sb("product", [P, TC, H], BF16)
        higher = sb("higher", [P, TC, S + P], BF16)
        score = sb("score", [P, TC])
        count = sb("count", [P, TC, 3])
        rank = sb("rank", [P, TC])
        routed = sb("routed", [P, TC])
        passed = sb("passed", [P, TC])
        base = sb("base", [P, TC, H])
        gate_in = sb("gate_in", [P, 2, 2 * H])
        h_sig = sb("h_sig", [P, 2, 2 * H])
        h_out = sb("h_out", [P, TC, H])
        y_out = sb("y_out", [P, TC, H])

        ps_s = ctx.enter_context(nc.psum_tensor("ps_s", [P, 2, 2 * S], F32))
        ps_o = ctx.enter_context(nc.psum_tensor("ps_o", [P, S], F32))
        ps_m = [ctx.enter_context(nc.psum_tensor(f"ps_m{i}", [P, S], F32)) for i in range(3)]

        weight_in = [sem(f"weight_in{i}") for i in range(5)]
        wr_in = sem("wr_in")
        weight_hi = sem("weight_hi")
        weight_lo = sem("weight_lo")
        x_loaded = sem("x_loaded")
        turned = sem("turned")
        spilled = [sem(f"spilled{i}") for i in range(4)]
        stacked = [sem(f"stacked{i}") for i in range(4)]
        zeros_set = sem("zeros_set")
        consts = sem("consts")
        hi = {k: sem(f"{k}_hi") for k in ("nt", "at", "xt")}
        scored = sem("scored")
        ready = {k: sem(f"{k}_ready") for k in PER}
        taken = {k: sem(f"{k}_taken") for k in PER}
        scores_done = sem("scores_done")
        sigmoid_done = sem("sigmoid_done")
        av_done = sem("av_done")
        v_set = sem("v_set")
        o_taken = sem("o_taken")
        part1 = sem("part1")
        part2 = sem("part2")
        part3 = sem("part3")
        stats1_done = sem("stats1_done")
        rstd1_done = sem("rstd1_done")
        ln1_done = sem("ln1_done")
        stats2_done = sem("stats2_done")
        rstd2_done = sem("rstd2_done")
        ln2_done = sem("ln2_done")
        den_done = sem("den_done")
        rank_done = sem("rank_done")
        base_done = sem("base_done")
        square_done = sem("square_done")
        arg_done = sem("arg_done")
        gate_done = sem("gate_done")
        out_ready = sem("out_ready")

        WEIGHTS = [(wq, wq_t), (wk, wk_t), (wv, wv_t), (wo, wo_t), (wb, w_block)]
        raw = [pr[:, 0, 0, :].rearrange("p (c o) -> p c o", c=4)[:, 0:2, :],
               pr[:, 0, 0, :].rearrange("p (c o) -> p c o", c=4)[:, 2:4, :],
               pr[:, 0, 1, :].rearrange("p (c o) -> p c o", c=4)[:, 0:2, :],
               pr[:, 0, 1, :].rearrange("p (c o) -> p c o", c=4)[:, 2:4, :],
               pr[:, 0, 2, :].rearrange("p (c o) -> p c o", c=4)[:, 0:2, :]]

        def to_view(bank):
            return ps_m[bank][:, :].rearrange("p (m w) -> p m w", w=VW)

        BANK = {(k, i): bank for _, k, i, bank, _ in JOBS}

        def has(step, off):
            return 0 <= step + off < B

        def last_user(step, flags, n):
            bank = JOBS[n][3]
            for m in reversed(range(n)):
                if JOBS[m][3] == bank and flags[JOBS[m][4]]:
                    return JOBS[m], 0
            if isinstance(step, int) and step - 1 < -1:
                return None
            before_flags = {-1: False, 0: False, 1: False}
            for off in (-1, 0, 1):
                before_flags[off] = has(step - 1, off) if isinstance(step, int) else off >= 0
            for m in reversed(range(len(JOBS))):
                if JOBS[m][3] == bank and before_flags[JOBS[m][4]]:
                    return JOBS[m], -1
            return None

        block = ctx.enter_context(nc.Block())

        def run_steps(eng, step):
            def flags(b):
                return {off: has(b, off) for off in (-1, 0, 1)}
            step(-1, flags(-1))
            step(0, flags(0))
            with eng.Fori(1, B - 1) as b:
                step(b, flags(1))
            step(B - 1, flags(B - 1))
            step(B, flags(B))

        @block.sync
        def _(sp):
            def load_x(b):
                sp.dma_start(x_in[:, :, :], x_d[b]).then_inc(x_loaded, 16)

            sp.dma_start(x_in[:, :, :], x_d[0]).then_inc(x_loaded, 16)
            for i, (_, w_d) in enumerate(WEIGHTS):
                sp.dma_start(raw[i], w_d.rearrange("(c p) o -> p c o", p=P)).then_inc(weight_in[i], 16)
            sp.dma_start(wr[:, :], w_router.rearrange("(a h) -> a h", a=1).broadcast_to([P, H])).then_inc(wr_in, 16)

            def spill(value, i):
                sp.wait_ge(part3, value["split", i])
                if value["read", i] is not None:
                    sp.wait_ge(stacked[i], value["read", i])
                sp.dma_start(parts[i].rearrange("t p n -> p t n"), split[:, i, :, :]).then_inc(spilled[i], 16)

            def stack(value, i):
                half, dst, order = i // 2, (q_st, k_st)[i % 2], (Q_PART, K_PART)[i % 2]
                sp.wait_ge(spilled[i], value["spilled", i])
                if value["scored", i] is not None:
                    sp.wait_ge(scores_done, value["scored", i])
                for s, part in enumerate(order):
                    sp.dma_start(dst[s * D:(s + 1) * D, half * HALF:(half + 1) * HALF, :],
                                 parts[i, part].rearrange("(h d) n -> d h n", d=D)).then_inc(stacked[i], 16)

            def values(b, on):
                value = {}
                for i, off in ((2, 0), (3, 0), (0, 1), (1, 1)):
                    if not on[off]:
                        continue
                    m = b + off
                    first = isinstance(m, int) and m == 0
                    value["split", i] = nth(m, 4, i)
                    value["read", i] = None if first else m * (16 * SLOTS)
                    value["spilled", i] = m * 16 + 16
                    value["scored", i] = None if first else (m - 1) * UNITS + (i // 2 + 1) * UNITS // 2
                if on[1] and not (isinstance(b, int) and b == -1):
                    value["normed"] = nth(b, 1)
                if on[0] and not (isinstance(b, int) and b == 0):
                    value["based"] = nth(b - 1, 2, 1)
                if on[-1]:
                    value["out", 0], value["out", 1] = nth(b - 1, 2, 0), nth(b - 1, 2, 1)
                if not isinstance(b, int):
                    value = {k: sp.to_reg(v) if v is not None else None for k, v in value.items()}
                return value

            def step(b, on):
                value = values(b, on)
                if "normed" in value:
                    sp.wait_ge(ln1_done, value["normed"])
                    load_x(b + 1)
                if on[0]:
                    spill(value, 2)
                    stack(value, 2)
                    spill(value, 3)
                    stack(value, 3)
                if on[1]:
                    spill(value, 0)
                    spill(value, 1)
                    stack(value, 0)
                    stack(value, 1)
                if on[0]:
                    if "based" in value:
                        sp.wait_ge(base_done, value["based"])
                    sp.dma_start(x1[:, :, :], x_d[b]).then_inc(turned, 16)
                if on[-1]:
                    for i in range(2):
                        sp.wait_ge(out_ready, value["out", i])
                        sp.dma_start(out_d[b - 1, :, 2 * i:2 * i + 2], y_out[:, 2 * i:2 * i + 2, :]).then_inc(turned, 16)

            run_steps(sp, step)
            sp.wait_ge(turned, 16 * 3 * B)

        @block.tensor
        def _(pe):
            def transposes(bank, src, c):
                for s in range(TC):
                    mm = nc.tensor.transpose(ps_m[bank][:, s * P:(s + 1) * P], src[:, s, c * P:(c + 1) * P],
                                             ident[:, :])
                return mm

            def product(ps_out, left, right):
                for c in range(HC):
                    for n, (l, r) in enumerate(PASSES):
                        mm = nc.tensor.matmul(ps_out, left(l, c), right(r, c), start=c == 0 and n == 0,
                                              stop=c == HC - 1 and n == len(PASSES) - 1)
                return mm

            def job(b, n, on):
                _, kind, i, bank, off = JOBS[n]
                if not on[off]:
                    return
                m = b + off
                user = last_user(b, on, n)
                if user is not None:
                    (_, k2, i2, _, off2), back = user
                    pe.wait_ge(taken[k2], nth(b + back + off2, PER[k2], i2))
                ps = ps_m[bank]
                if kind == "nt":
                    pe.wait_ge(ln1_done, nth(m, 1))
                    mm = transposes(bank, xn, i)
                elif kind == "qk":
                    w, half = (wq, wk)[i % 2], i // 2
                    pe.wait_ge(taken["nt"], nth(m, 2, 1))
                    mm = product(ps[:, :], lambda a, c: w[:, a, c, half * P:(half + 1) * P],
                                 lambda a, c: xn_t[:, a, c, :])
                elif kind == "v":
                    pe.wait_ge(taken["nt"], nth(m, 2, 1))
                    for s in range(2):
                        t = 2 * i + s
                        mm = product(ps[:, s * H:(s + 1) * H], lambda a, c: xn_t[:, a, c, t * P:(t + 1) * P],
                                     lambda a, c: wv[:, a, c, :])
                elif kind == "to":
                    pe.wait_ge(o_taken, nth(m, GROUPS, i))
                    for s in range(TC):
                        mm = nc.tensor.transpose(ps[:, s * P:(s + 1) * P], o_t[:, i % 2, s * P:(s + 1) * P],
                                                 ident[:, :])
                elif kind == "at":
                    pe.wait_ge(taken["to"], nth(m, GROUPS, GROUPS - 1))
                    mm = transposes(bank, att, i)
                elif kind == "y":
                    pe.wait_ge(taken["at"], nth(m, 2, 1))
                    for s in range(2):
                        t = 2 * i + s
                        mm = product(ps[:, s * H:(s + 1) * H], lambda a, c: att_t[:, a, c, t * P:(t + 1) * P],
                                     lambda a, c: wo[:, a, c, :])
                elif kind == "xt":
                    pe.wait_ge(ln2_done, nth(m, 1))
                    mm = transposes(bank, xn2, i)
                elif kind == "sc":
                    pe.wait_ge(scored, nth(m, 1))
                    for t in range(TC):
                        mm = nc.tensor.transpose(ps[:, t * P:(t + 1) * P],
                                                 score[:, t:t + 1].broadcast_to([P, P]), ident[:, :])
                elif kind == "h":
                    pe.wait_ge(taken["xt"], nth(m, 2, 1))
                    for s in range(2):
                        t = 2 * i + s
                        mm = product(ps[:, s * H:(s + 1) * H], lambda a, c: xn2_t[:, a, c, t * P:(t + 1) * P],
                                     lambda a, c: wb[:, a, c, :])
                mm.then_inc(ready[kind], 1)

            def scores(b, n):
                g, p, j = n // 8, n // 4 % 2, n % 4
                h = GROUP * g + j
                if n % (UNITS // 2) == 0:
                    for i in (2 * (n * 2 // UNITS), 2 * (n * 2 // UNITS) + 1):
                        pe.wait_ge(stacked[i], (b + 1) * (16 * SLOTS))
                if not (isinstance(b, int) and b == 0 and n < 2):
                    pe.wait_ge(sigmoid_done, b * UNITS + n - 1)
                for kk in range(2):
                    kc = 2 * p + kk
                    mm = nc.tensor.matmul(ps_s[:, n % 2, kk * S:(kk + 1) * S], k_st[:, h, kc * P:(kc + 1) * P],
                                          q_st[:, h, :], start=True, stop=True)
                mm.then_inc(scores_done, 1)

            def weighted_sum(b, r, kk):
                g, p = r // 2, r % 2
                kc = 2 * p + kk
                if kk == 0:
                    pe.wait_ge(sigmoid_done, b * UNITS + 4 * r + 4)
                    if p == 0:
                        if g % 2 == 0:
                            pe.wait_ge(v_set, nth(b, 2, g // 2))
                        if not (isinstance(b, int) and b == 0 and g == 0):
                            pe.wait_ge(o_taken, b * GROUPS + g)
                for j in range(GROUP):
                    mm = nc.tensor.matmul(ps_o[j * VW:(j + 1) * VW, :], v_x[:, kc, GROUP * g + j, :],
                                          pr[:, p, j, kk * S:(kk + 1) * S], start=kc == 0, stop=kc == TC - 1)
                mm.then_inc(av_done, 1)

            def step(b, on):
                for n in range(UNITS):
                    if on[0]:
                        scores(b, n)
                    if n % 2 == 1:
                        r, kk = n // 4 - 1, n % 4 // 2
                        if r < 0 and on[-1]:
                            weighted_sum(b - 1, r + 2 * GROUPS, kk)
                        if r >= 0 and on[0]:
                            weighted_sum(b, r, kk)
                    for m in range(len(JOBS)):
                        if JOBS[m][0] == n:
                            job(b, m, on)

            pe.wait_ge(consts, 1)
            pe.wait_ge(weight_lo, len(WEIGHTS))
            run_steps(pe, step)

        @block.scalar
        def _(act):
            def hi_part(kind, b, i, dst):
                act.wait_ge(ready[kind], nth(b, PER[kind], i))
                nc.scalar.copy(dst[:, 0, i, :], ps_m[BANK[kind, i]][:, :]).then_inc(hi[kind], 1)

            def take_scores(b):
                act.wait_ge(ready["sc"], nth(b, 1))
                nc.scalar.copy(s_row[:, :], ps_m[BANK["sc", 0]][:, :]).then_inc(taken["sc"], 1)

            def first_part(b, i):
                act.wait_ge(ready["qk"], nth(b, 4, i))
                if not (isinstance(b, int) and b == 0):
                    act.wait_ge(spilled[i], b * 16)
                nc.scalar.copy(split[:, i, 0, :], ps_m[BANK["qk", i]][:, :]).then_inc(part1, 1)

            def values(b, i):
                act.wait_ge(ready["v"], nth(b, 2, i))
                if not (isinstance(b, int) and b == 0):
                    act.wait_ge(v_set, b * 2)
                nc.scalar.copy(v_in[:, 2 * i:2 * i + 2, :],
                               ps_m[BANK["v", i]][:, :].rearrange("p (t h) -> p t h", t=2)).then_inc(taken["v"], 1)

            def take_o(b, g):
                act.wait_ge(av_done, nth(b, 4 * GROUPS, 4 * g + 3))
                if not (isinstance(b, int) and b == 0 and g < 2):
                    act.wait_ge(ready["to"], b * GROUPS + g - 1)
                nc.scalar.copy(o_t[:, g % 2, :], ps_o[:, :]).then_inc(o_taken, 1)

            def sigmoid(b, n):
                r, j = n // 4, n % 4
                act.wait_ge(scores_done, b * UNITS + n + 1)
                if j == 0 and not (isinstance(b, int) and b == 0 and r < 2):
                    act.wait_ge(av_done, b * 4 * GROUPS + 2 * (r - 1))
                nc.scalar.activation(pr[:, r % 2, j, :], ps_s[:, n % 2, :], ACT.Sigmoid,
                                     scale=SCALE).then_inc(sigmoid_done, 1)

            def square(b, i):
                act.wait_ge(ready["h"], nth(b, 2, i))
                nc.scalar.activation(gate_in[:, i, :], ps_m[BANK["h", i]][:, :], ACT.Square).then_inc(square_done, 1)

            def gate(b, i):
                act.wait_ge(arg_done, nth(b, 2, i))
                nc.scalar.activation(h_sig[:, i, :], gate_in[:, i, :], ACT.Sigmoid,
                                     scale=GELU_G * GELU_A).then_inc(gate_done, 1)

            def step(b, on):
                for n in range(UNITS):
                    if on[0]:
                        sigmoid(b, n)
                        if n == 2:
                            first_part(b, 2)
                        if n == 7:
                            first_part(b, 3)
                        if n == 11:
                            take_o(b, 0)
                        if n == 19:
                            take_o(b, 1)
                        if n == 27:
                            take_o(b, 2)
                    if on[-1]:
                        if n == 3:
                            take_o(b - 1, 3)
                        if n == 9:
                            hi_part("at", b - 1, 0, att_t)
                        if n == 10:
                            hi_part("at", b - 1, 1, att_t)
                        if n == 20:
                            hi_part("xt", b - 1, 0, xn2_t)
                        if n == 21:
                            hi_part("xt", b - 1, 1, xn2_t)
                        if n == 22:
                            take_scores(b - 1)
                        if n == 25:
                            square(b - 1, 0)
                        if n == 26:
                            gate(b - 1, 0)
                        if n == 27:
                            square(b - 1, 1)
                        if n == 28:
                            gate(b - 1, 1)
                    if on[1]:
                        if n == 11:
                            hi_part("nt", b + 1, 0, xn_t)
                        if n == 12:
                            hi_part("nt", b + 1, 1, xn_t)
                        if n == 16:
                            first_part(b + 1, 0)
                        if n == 18:
                            first_part(b + 1, 1)
                        if n == 29:
                            values(b + 1, 0)
                        if n == 30:
                            values(b + 1, 1)

            for i, (w, _) in enumerate(WEIGHTS):
                act.wait_ge(weight_in[i], 16)
                nc.scalar.copy(w[:, 0, :, :], raw[i]).then_inc(weight_hi, 1)
            run_steps(act, step)

        @block.vector
        def _(dve):
            def chunk_stats(src, stats, chunks):
                for s in chunks:
                    op = nc.vector.bn_stats(stats[:, s, :], src[:, s, :])
                return op

            def row_stats(b, stats, mv, mean, ve, stats_done):
                dve.wait_ge(stats_done, nth(b, 4, 0))
                m0, s0, m1, s1 = (stats[:, :, k] for k in (1, 2, 4, 5))
                nc.vector.tensor_tensor(mv[:, :, 0], m0, m1, ALU.add)
                nc.vector.tensor_tensor(mv[:, :, 1], m0, m1, ALU.subtract)
                nc.vector.tensor_tensor(mv[:, :, 2], s0, s1, ALU.add).then_inc(stats_done, 1)
                dve.wait_ge(stats_done, nth(b, 4, 1))
                nc.vector.tensor_scalar(mean[:, :], mv[:, :, 0], 0.5, None, ALU.mult)
                nc.vector.tensor_scalar(mv[:, :, 3], mv[:, :, 2], 1.0 / H, EPS_LN, ALU.mult, ALU.add)
                nc.vector.scalar_tensor_tensor(mv[:, :, 4], mv[:, :, 1], 0.25, mv[:, :, 1],
                                               ALU.mult, ALU.mult).then_inc(stats_done, 1)
                dve.wait_ge(stats_done, nth(b, 4, 2))
                nc.vector.tensor_tensor(ve[:, :], mv[:, :, 3], mv[:, :, 4], ALU.add).then_inc(stats_done, 1)

            def row_norm(b, src, mean, rstd, rstd_done, dst, done):
                dve.wait_ge(rstd_done, nth(b, 1))
                for s in range(TC):
                    op = nc.vector.tensor_scalar(dst[:, s, :], src[:, s, :], mean[:, s:s + 1], rstd[:, s:s + 1],
                                                 ALU.subtract, ALU.mult)
                op.then_inc(done, 1)

            def stats_1(b):
                dve.wait_ge(x_loaded, 16 * b + 16)
                chunk_stats(x_in, stats1, range(TC)).then_inc(stats1_done, 1)
                row_stats(b, stats1, mv1, mean1, ve1, stats1_done)

            def norm_1(b, first):
                if not first:
                    dve.wait_ge(ready["nt"], nth(b - 1, 2, 1))
                row_norm(b, x_in, mean1, rstd1, rstd1_done, xn, ln1_done)

            def stats_2(b):
                for i in range(2):
                    residual(b, i)
                    dve.wait_ge(taken["y"], nth(b, 2, i))
                    op = chunk_stats(x1, stats2, (2 * i, 2 * i + 1))
                op.then_inc(stats2_done, 1)
                row_stats(b, stats2, mv2, mean2, ve2, stats2_done)

            def norm_2(b):
                row_norm(b, x1, mean2, rstd2, rstd2_done, xn2, ln2_done)

            def router(b):
                dve.wait_ge(ln2_done, nth(b, 1))
                for t in range(TC):
                    op = nc.vector.tensor_tensor_reduce(product[:, t, :], xn2[:, t, :], wr[:, :], 1.0, 0.0,
                                                        ALU.mult, ALU.add, score[:, t:t + 1])
                op.then_inc(scored, 1)

            def lo_part(kind, b, i, dst):
                dve.wait_ge(hi[kind], nth(b, 2, i))
                nc.vector.tensor_tensor(dst[:, 1, i, :], ps_m[BANK[kind, i]][:, :], dst[:, 0, i, :].bitcast(F32),
                                        ALU.subtract).then_inc(taken[kind], 1)

            def split_rest(b, i):
                dve.wait_ge(part1, nth(b, 4, i))
                if not (isinstance(b, int) and b == 0):
                    dve.wait_ge(part3, nth(b - 1, 4, i))
                nc.vector.tensor_tensor(rest[:, i, :], ps_m[BANK["qk", i]][:, :], split[:, i, 0, :],
                                        ALU.subtract).then_inc(taken["qk"], 1)
                dve.wait_ge(taken["qk"], nth(b, 4, i))
                nc.vector.tensor_copy(split[:, i, 1, :], rest[:, i, :]).then_inc(part2, 1)

            def normalise(b, g):
                view = to_view(BANK["to", g])
                dve.wait_ge(ready["to"], nth(b, GROUPS, g))
                nc.vector.tensor_scalar(den[:, g, :], view[:, :, D], EPS_W, None, ALU.add).then_inc(den_done, 1)
                dve.wait_ge(den_done, nth(b, 2 * GROUPS, 2 * g))
                nc.vector.reciprocal(rden[:, g, :], den[:, g, :]).then_inc(den_done, 1)
                dve.wait_ge(den_done, nth(b, 2 * GROUPS, 2 * g + 1))
                if g == 0 and not (isinstance(b, int) and b == 0):
                    dve.wait_ge(ready["at"], nth(b - 1, 2, 1))
                w = GROUP * D
                nc.vector.tensor_tensor(
                    att[:, :, g * w:(g + 1) * w].rearrange("p t (j d) -> p t j d", d=D),
                    view[:, :, 0:D].rearrange("p (t j) d -> p t j d", t=TC),
                    rden[:, g, :].rearrange("p (t j) -> p t j", t=TC).unsqueeze(3).broadcast_to([P, TC, GROUP, D]),
                    ALU.mult).then_inc(taken["to"], 1)

            def set_values(b, i):
                dve.wait_ge(taken["v"], nth(b, 2, 1))
                if not (isinstance(b, int) and b == 0):
                    dve.wait_ge(av_done, (b - 1) * 4 * GROUPS + (i + 1) * 2 * GROUPS)
                nc.vector.tensor_copy(v_x[:, :, i * HALF:(i + 1) * HALF, 0:D],
                                      v_in[:, :, i * P:(i + 1) * P].rearrange("p t (h d) -> p t h d", d=D)
                                      ).then_inc(v_set, 1)

            def residual(b, i):
                dve.wait_ge(ready["y"], nth(b, 2, i))
                dve.wait_ge(turned, 48 * b + 16)
                nc.vector.tensor_tensor(x1[:, 2 * i:2 * i + 2, :],
                                        ps_m[BANK["y", i]][:, :].rearrange("p (t h) -> p t h", t=2),
                                        x1[:, 2 * i:2 * i + 2, :], ALU.add).then_inc(taken["y"], 1)

            def count_higher(b):
                dve.wait_ge(taken["sc"], nth(b, 1))
                for t in range(TC):
                    own = score[:, t:t + 1]
                    if t > 0:
                        nc.vector.tensor_scalar(higher[:, t, 0:t * P], s_row[:, 0:t * P], own, None, ALU.is_ge,
                                                ALU.add, accum_out=count[:, t, 0:1])
                    nc.vector.tensor_scalar(higher[:, t, t * P:S], s_row[:, t * P:S], own, None, ALU.is_gt, ALU.add,
                                            accum_out=count[:, t, 1:2])
                    op = nc.vector.scalar_tensor_tensor(higher[:, t, S:S + P], s_row[:, t * P:(t + 1) * P], own,
                                                        before[:, :], ALU.is_equal, ALU.mult,
                                                        accum_out=count[:, t, 2:3])
                op.then_inc(rank_done, 1)

            def choose(b):
                dve.wait_ge(rank_done, nth(b, 4, 0))
                nc.vector.tensor_reduce(rank[:, :], count[:, :, :], AX_X, ALU.add).then_inc(rank_done, 1)
                dve.wait_ge(rank_done, nth(b, 4, 1))
                nc.vector.tensor_scalar(routed[:, :], rank[:, :], float(TOP), None, ALU.is_lt).then_inc(rank_done, 1)
                nc.vector.tensor_scalar(passed[:, :], rank[:, :], float(TOP), None, ALU.is_ge).then_inc(rank_done, 1)

            def residual_base(b, i):
                dve.wait_ge(rank_done, nth(b, 4, 3))
                for t in (2 * i, 2 * i + 1):
                    op = nc.vector.scalar_tensor_tensor(base[:, t, :], xn2[:, t, :], passed[:, t:t + 1], x1[:, t, :],
                                                        ALU.mult, ALU.add)
                op.then_inc(base_done, 1)

            def gelu_arg(b, i):
                dve.wait_ge(square_done, nth(b, 2, i))
                nc.vector.scalar_tensor_tensor(gate_in[:, i, :], gate_in[:, i, :], 1.0 / GELU_A,
                                               ps_m[BANK["h", i]][:, :], ALU.add, ALU.mult).then_inc(arg_done, 1)

            def gelu(b, i):
                dve.wait_ge(gate_done, nth(b, 2, i))
                dve.wait_ge(rank_done, nth(b, 4, 3))
                for s in range(2):
                    t = 2 * i + s
                    op = nc.vector.scalar_tensor_tensor(h_out[:, t, :], h_sig[:, i, s * H:(s + 1) * H],
                                                        routed[:, t:t + 1],
                                                        ps_m[BANK["h", i]][:, s * H:(s + 1) * H],
                                                        ALU.mult, ALU.mult)
                op.then_inc(taken["h"], 1)

            def step(b, on):
                if on[0]:
                    split_rest(b, 2)
                if on[-1]:
                    normalise(b - 1, 3)
                if on[0]:
                    set_values(b, 1)
                if on[1] and not (isinstance(b, int) and b == -1):
                    stats_1(b + 1)
                if on[0]:
                    split_rest(b, 3)
                if on[1] and not (isinstance(b, int) and b == -1):
                    norm_1(b + 1, False)
                if on[-1]:
                    lo_part("at", b - 1, 0, att_t)
                    lo_part("at", b - 1, 1, att_t)
                if on[1]:
                    lo_part("nt", b + 1, 0, xn_t)
                    lo_part("nt", b + 1, 1, xn_t)
                if on[-1]:
                    stats_2(b - 1)
                if on[0]:
                    normalise(b, 0)
                if on[1]:
                    split_rest(b + 1, 0)
                if on[-1]:
                    norm_2(b - 1)
                    router(b - 1)
                if on[1]:
                    split_rest(b + 1, 1)
                if on[-1]:
                    lo_part("xt", b - 1, 0, xn2_t)
                    lo_part("xt", b - 1, 1, xn2_t)
                    count_higher(b - 1)
                if on[0]:
                    normalise(b, 1)
                if on[-1]:
                    gelu_arg(b - 1, 0)
                    choose(b - 1)
                    residual_base(b - 1, 0)
                    gelu(b - 1, 0)
                    gelu_arg(b - 1, 1)
                    residual_base(b - 1, 1)
                    gelu(b - 1, 1)
                if on[0]:
                    normalise(b, 2)
                if on[1]:
                    set_values(b + 1, 0)

            stats_1(0)
            for i, (w, _) in enumerate(WEIGHTS):
                if i == 2:
                    norm_1(0, True)
                dve.wait_ge(weight_hi, i + 1)
                nc.vector.tensor_tensor(w[:, 1, :, :], raw[i], w[:, 0, :, :].bitcast(F32),
                                        ALU.subtract).then_inc(weight_lo, 1)
            dve.wait_ge(consts, 1)
            dve.wait_ge(wr_in, 16)
            run_steps(dve, step)

        @block.gpsimd
        def _(pool):
            nc.gpsimd.memset(ident[:, :], 0.0)
            nc.gpsimd.memset(before[:, :], 0.0)
            nc.gpsimd.memset(minus_half[:, :], -0.5)
            nc.gpsimd.memset(count[:, :, :], 0.0)
            nc.gpsimd.memset(v_x[:, :, :, :], 1.0).then_inc(zeros_set, 1)
            pool.wait_ge(zeros_set, 1)
            nc.gpsimd.affine_select(out=ident[:, :], in_=ident[:, :], compare_op=ALU.not_equal, fill=1.0,
                                    base=0, pattern=[[-1, P]], channel_multiplier=1)
            nc.gpsimd.affine_select(out=before[:, :], in_=before[:, :], compare_op=ALU.is_ge, fill=1.0,
                                    base=0, pattern=[[1, P]], channel_multiplier=-1).then_inc(consts, 1)

            def third_part(b, i):
                pool.wait_ge(part2, nth(b, 4, i))
                nc.gpsimd.tensor_tensor(split[:, i, 2, :], rest[:, i, :], split[:, i, 1, :],
                                        ALU.subtract).then_inc(part3, 1)

            def inverse_root(b, ve, rstd, stats_done, rstd_done):
                pool.wait_ge(stats_done, nth(b, 4, 3))
                nc.gpsimd.tensor_tensor(rstd[:, :], ve[:, :], minus_half[:, :], ALU.pow).then_inc(rstd_done, 1)

            def output(b, i):
                pool.wait_ge(base_done, nth(b, 2, i))
                pool.wait_ge(turned, 48 * b + 16)
                pool.wait_ge(taken["h"], nth(b, 2, i))
                chunks = slice(2 * i, 2 * i + 2)
                nc.gpsimd.tensor_tensor(y_out[:, chunks, :], base[:, chunks, :], h_out[:, chunks, :],
                                        ALU.add).then_inc(out_ready, 1)

            def step(b, on):
                if on[0]:
                    third_part(b, 2)
                if on[1]:
                    inverse_root(b + 1, ve1, rstd1, stats1_done, rstd1_done)
                if on[0]:
                    third_part(b, 3)
                if on[-1]:
                    inverse_root(b - 1, ve2, rstd2, stats2_done, rstd2_done)
                if on[1]:
                    third_part(b + 1, 0)
                    third_part(b + 1, 1)
                if on[-1]:
                    output(b - 1, 0)
                    output(b - 1, 1)

            run_steps(pool, step)


def kernel(**inputs):
    import numpy as _np
    import concourse.bacc as _bacc
    from concourse import mybir as _mybir
    from concourse.bass_utils import run_bass_kernel_spmd as _run

    nc = _bacc.Bacc("TRN2", target_bir_lowering=False, num_devices=1)
    arrays, args = {}, []
    for name in ("L0_attn_x", "L0_attn_Wq", "L0_attn_Wk", "L0_attn_Wv", "L0_attn_Wo",
                 "L0_ffn_w_router", "L0_ffn_w_block"):
        a = _np.asarray(inputs[name])
        if name.startswith("L0_attn_W"):
            a = a.T
        a = _np.ascontiguousarray(a)
        arrays[f"in_{name}"] = a
        args.append(nc.dram_tensor(f"in_{name}", a.shape, _mybir.dt.from_np(a.dtype), kind="ExternalInput").ap())
    args.append(nc.dram_tensor("out_0", (B, S, H), F32, kind="ExternalOutput").ap())
    layer(nc, *args)
    r = _run(nc, [arrays], core_ids=[0])
    return r.results[0]["out_0"]
```

```python
from contextlib import ExitStack

import concourse.bass as bass
from concourse import mybir

F32 = mybir.dt.float32
F32R = mybir.dt.float32r
BF16 = mybir.dt.bfloat16
ALU = mybir.AluOpType
ACT = mybir.ActivationFunctionType
AX_X = mybir.AxisListType.X

P = 128
B, S, H = 8, 512, 256
HEADS = 16
D = H // HEADS
TC = S // P
HC = H // P
SCALE = float(D) ** -0.5
EPS_W = 1e-6
EPS_LN = 1e-5
TOP = int(S * 0.75)
GROUP = 4
GROUPS = HEADS // GROUP
VW = 32
HALF = HEADS // 2
UNITS = HEADS * 2
RUNS = (2, 1)
SLOTS = sum(RUNS)
PARTS = 2
TILE = 64
STACKED = 16 * 2 * len(RUNS)
GELU_A = 0.044715
GELU_G = 1.5957691216057308

JOB_LIST = [
    (0, "qk", 2, 0),
    (6, "qk", 3, 0),
    (9, "y", 0, -1),
    (10, "y", 1, -1),
    (12, "nt", 0, 1),
    (13, "nt", 1, 1),
    (15, "xt", 0, -1),
    (16, "xt", 1, -1),
    (17, "sc", 0, -1),
    (18, "qk", 0, 1),
    (18, "h", 0, -1),
    (21, "h", 1, -1),
    (22, "qk", 1, 1),
    (26, "v", 0, 1),
    (30, "v", 1, 1),
]
MISC_BANKS = 3
JOBS = [(n, kind, i, m % MISC_BANKS, off) for m, (n, kind, i, off) in enumerate(JOB_LIST)]
assert len(JOBS) % MISC_BANKS == 0
*TAKE_O, HI_0, HI_1, GATE_LAG = [11, 19, 27, 3, 26, 6, 3]
BLOCK = 32
BLOCKS = S // BLOCK


def jobs_of(step):
    if not isinstance(step, int):
        return JOBS
    early = [job for job in JOBS if job[1] == "qk" and job[4] == 0]
    if step == -1:
        return [job for job in JOBS if job[4] == 1] + [(UNITS - 1, k, i, bank, 1) for _, k, i, bank, _ in early]
    return [job for job in JOBS if 0 <= step + job[4] < B and not (step == 0 and job in early)]


PER = {"qk": 4, "v": 2, "y": 2, "nt": 2, "xt": 2, "sc": 1, "h": 2}
PASSES = ((0, 0), (0, 1), (1, 0))


def nth(b, per, i=0):
    return b * per + i + 1


def layer(nc, x, wq_t, wk_t, wv_t, wo_t, w_router, w_block, out):
    parts = nc.dram_tensor("qk_parts", (4 * PARTS + 2, P, S), F32, kind="Internal").ap()
    x_d = x.rearrange("b (s p) h -> b p s h", p=P)
    out_d = out.rearrange("b (s p) h -> b p s h", p=P)

    with ExitStack() as ctx:
        def sb(name, shape, dt=F32):
            return ctx.enter_context(nc.sbuf_tensor(name, shape, dt))

        def sem(name):
            return ctx.enter_context(nc.semaphore(name))

        wq, wk, wv, wo, wb = (sb(name, [P, 2, HC, H], F32R) for name in ("wq", "wk", "wv", "wo", "wb"))
        wr = sb("wr", [P, H])
        ident = sb("ident", [P, P])
        before = sb("before", [P, P])
        minus_half = sb("minus_half", [P, TC])
        x_in = sb("x_in", [P, TC, H])
        xn = sb("xn", [P, TC, H])
        xn_t = sb("xn_t", [P, 2, HC, S], F32R)
        stats1 = sb("stats1", [P, TC, 6])
        mv1 = sb("mv1", [P, TC, 5])
        mean1 = sb("mean1", [P, TC])
        ve1 = sb("ve1", [P, TC])
        rstd1 = sb("rstd1", [P, TC])
        split = sb("split", [P, 4, PARTS, S], F32R)
        qk_st = sb("qk_st", [TILE + SLOTS * D, 2, HEADS // 2, S], F32R)
        q_st, k_st = qk_st[:, 0], qk_st[:, 1]
        v_in = sb("v_in", [P, TC, H - P])
        v_x = sb("v_x", [P, TC, HEADS, VW])
        pr = sb("pr", [P, 2, 2, GROUP, S])
        o_t = sb("o_t", [P, 2, S])
        o_x = sb("o_x", [P, BLOCKS, VW])
        att_x = sb("att_x", [P, BLOCKS, 2, D])
        den = sb("den", [P, GROUPS, BLOCKS])
        rden = sb("rden", [P, GROUPS, BLOCKS])
        att = sb("att", [P, HC, S])
        att_t = sb("att_t", [P, 2, HC, S], F32R)
        x1 = sb("x1", [P, TC, H])
        xn2 = sb("xn2", [P, TC, H])
        xn2_t = sb("xn2_t", [P, 2, HC, S], F32R)
        stats2 = sb("stats2", [P, TC, 6])
        mv2 = sb("mv2", [P, TC, 5])
        mean2 = sb("mean2", [P, TC])
        ve2 = sb("ve2", [P, TC])
        rstd2 = sb("rstd2", [P, TC])
        product = sb("product", [P, TC, H], BF16)
        higher = sb("higher", [P, TC, S + P], BF16)
        score = sb("score", [P, TC])
        s_row = sb("s_row", [P, S])
        count = sb("count", [P, TC, 3])
        rank = sb("rank", [P, TC])
        routed = sb("routed", [P, TC])
        passed = sb("passed", [P, TC])
        base = sb("base", [P, TC, H])
        gate_in = sb("gate_in", [P, 2, 2 * H])
        h_sig = sb("h_sig", [P, 2, 2 * H])
        h_out = sb("h_out", [P, TC, H])
        y_out = sb("y_out", [P, TC, H])

        ps_s = ctx.enter_context(nc.psum_tensor("ps_s", [P, 2, 2 * S], F32))
        ps_o = ctx.enter_context(nc.psum_tensor("ps_o", [P, S], F32))
        ps_m = [ctx.enter_context(nc.psum_tensor(f"ps_m{i}", [P, S], F32)) for i in range(MISC_BANKS)]

        weight_in = [sem(f"weight_in{i}") for i in range(5)]
        wr_in = sem("wr_in")
        weight_hi = sem("weight_hi")
        weight_lo = sem("weight_lo")
        x_first = sem("x_first")
        x_loaded = sem("x_loaded")
        turned = sem("turned")
        spilled = [sem(f"spilled{i}") for i in range(2)]
        stacked = [sem(f"stacked{g}") for g in range(GROUPS)]
        zeros_set = sem("zeros_set")
        consts = sem("consts")
        hi = {k: sem(f"{k}_hi") for k in ("nt", "xt")}
        scored = sem("scored")
        ready = {k: sem(f"{k}_ready") for k in PER}
        taken = {k: sem(f"{k}_taken") for k in PER}
        scores_done = sem("scores_done")
        sigmoid_done = sem("sigmoid_done")
        av_done = sem("av_done")
        v_set = sem("v_set")
        o_taken = sem("o_taken")
        o_turned = sem("o_turned")
        att_set = sem("att_set")
        att_turned = sem("att_turned")
        att_hi = sem("att_hi")
        att_lo = sem("att_lo")
        part1 = sem("part1")
        stats1_done = sem("stats1_done")
        rstd1_done = sem("rstd1_done")
        ln1_done = sem("ln1_done")
        stats2_done = sem("stats2_done")
        rstd2_done = sem("rstd2_done")
        ln2_done = sem("ln2_done")
        den_done = sem("den_done")
        rank_done = sem("rank_done")
        base_done = sem("base_done")
        square_done = sem("square_done")
        arg_done = sem("arg_done")
        gate_done = sem("gate_done")
        out_ready = sem("out_ready")
        last_ready = sem("last_ready")

        WEIGHTS = [(wq, wq_t), (wk, wk_t), (wv, wv_t), (wo, wo_t), (wb, w_block)]
        raw = [pr[:, 0, i // GROUP, i % GROUP, :].rearrange("p (c o) -> p c o", c=HC) for i in range(len(WEIGHTS))]

        BANK = {(k, i): bank for _, k, i, bank, _ in JOBS}

        READY_WEIGHTS = {"qk": 2, "v": 3, "y": 4, "h": 5}
        WARM_START, WARM_SCORES, WARM_UNIT = 16, 15, 2
        WARM_JOBS = {("y", 0): 16, ("xt", 0): 18}

        def place(i, part):
            return part if i % 2 == 0 else 1 - part

        def split_part(i, part):
            return split[:, i, place(i, part), :]

        def has(step, off):
            return 0 <= step + off < B

        def last_user(step, n):
            jobs = jobs_of(step)
            for job in reversed(jobs[:n]):
                if job[3] == jobs[n][3]:
                    return job, 0
            before = jobs_of(0) if not isinstance(step, int) else [] if step == -1 else jobs_of(step - 1)
            for job in reversed(before):
                if job[3] == jobs[n][3]:
                    return job, -1
            return None

        block = ctx.enter_context(nc.Block())

        def run_steps(eng, step):
            def flags(b):
                return {off: has(b, off) for off in (-1, 0, 1)}
            step(-1, flags(-1))
            step(0, flags(0))
            with eng.Fori(1, B - 1) as b:
                step(b, flags(1))
            step(B - 1, flags(B - 1))
            step(B, flags(B))

        @block.sync
        def _(sp):
            def load_x(b):
                sp.dma_start(x_in[:, :, :], x_d[b]).then_inc(x_loaded, 16)

            for s, is_loaded in ((0, x_first), (2, x_loaded)):
                sp.dma_start(x_in[:, s:s + 2, :], x_d[0, :, s:s + 2]).then_inc(is_loaded, 16)
            for i, (_, w_d) in enumerate(WEIGHTS):
                sp.dma_start(raw[i], w_d.rearrange("(c p) o -> p c o", p=P)).then_inc(weight_in[i], 16)
            sp.dma_start(wr[:, :], w_router.rearrange("(a h) -> a h", a=1).broadcast_to([P, H])).then_inc(wr_in, 16)

            part_rows = parts.rearrange("t (d h) n -> (t d) h n", d=D)

            def spill(value, i):
                sp.wait_ge(taken["qk"], value["split", i])
                if i % 2 == 0:
                    for g in (i, i + 1):
                        sp.wait_ge(stacked[g], value["read", i // 2])
                sp.dma_start(parts[PARTS * i:PARTS * (i + 1)].rearrange("t p n -> p t n"),
                             split[:, i, :, :].bitcast(F32)).then_inc(spilled[i // 2], 16)

            def spill_first(i):
                for part, is_there in ((0, part1), (1, taken["qk"])):
                    sp.wait_ge(is_there, i + 1)
                    sp.dma_start(parts[PARTS * i + place(i, part)], split_part(i, part).bitcast(F32)
                                 ).then_inc(spilled[i // 2], 16)

            def stack(value, half):
                sp.wait_ge(spilled[half], value["spilled", half])
                for g in (2 * half, 2 * half + 1):
                    if value["scored", g] is not None:
                        sp.wait_ge(scores_done, value["scored", g])
                    pairs = slice(2 * g, 2 * g + 2)
                    for tile in range(2):
                        first_head = tile * HALF // 2 + 2 * (g % 2)
                        slot = 0
                        for run in RUNS:
                            first, apart = 2 * PARTS * half, 2 * PARTS - run
                            src = part_rows[first * D:(first + 2 * apart) * D].rearrange("(i r) h n -> r i h n", i=2)
                            row = tile * TILE + slot * D
                            sp.dma_start(qk_st[row:row + run * D, :, pairs, :].bitcast(F32)
                                         .rearrange("r i h n -> r i (h n)"),
                                         src[0:run * D, :, first_head:first_head + 2, :]
                                         .rearrange("r i h n -> r i (h n)")).then_inc(stacked[g], 16)
                            slot += run

            def values(b, on):
                value = {}
                first_batch = isinstance(b, int) and b == -1
                for half, off in ((1, 1 if first_batch else 0), (0, 1)):
                    if not on[off]:
                        continue
                    m = b + off
                    first = isinstance(m, int) and m == 0
                    value["split", 2 * half] = nth(m, 4, 2 * half)
                    value["split", 2 * half + 1] = nth(m, 4, 2 * half + 1)
                    value["read", half] = None if first else m * STACKED
                    value["spilled", half] = m * 32 + 64
                    for g in (2 * half, 2 * half + 1):
                        value["scored", g] = None if first else (m - 1) * UNITS + (g + 1) * UNITS // GROUPS
                if on[1] and not first_batch and not (isinstance(b, int) and b == 0):
                    value["normed"] = nth(b, 1)
                if on[0] and not (isinstance(b, int) and b == 0):
                    value["based"] = nth(b - 1, 2, 1)
                if on[-1]:
                    value["out", 0], value["out", 1] = nth(b - 1, 2, 0), nth(b - 1, 2, 1)
                if not isinstance(b, int):
                    value = {k: sp.to_reg(v) if v is not None else None for k, v in value.items()}
                return value

            def step(b, on):
                value = values(b, on)
                first_batch = isinstance(b, int) and b == -1
                if "normed" in value:
                    sp.wait_ge(ln1_done, value["normed"])
                    load_x(b + 1)
                if on[0] and not (isinstance(b, int) and b == 0):
                    spill(value, 2)
                    spill(value, 3)
                    stack(value, 1)
                if on[1] and not first_batch:
                    spill(value, 0)
                    spill(value, 1)
                    stack(value, 0)
                if first_batch:
                    spill_first(0)
                    spill_first(1)
                    stack(value, 0)
                    sp.wait_ge(ln1_done, 1)
                    load_x(1)
                    spill_first(2)
                    spill_first(3)
                    stack(value, 1)
                if on[0]:
                    if "based" in value:
                        sp.wait_ge(base_done, value["based"])
                    sp.dma_start(x1[:, :, :], x_d[b]).then_inc(turned, 16)
                if on[-1]:
                    for i in range(2):
                        if isinstance(b, int) and b == B and i == 1:
                            sp.wait_ge(last_ready, 1)
                        else:
                            sp.wait_ge(out_ready, value["out", i])
                        sp.dma_start(out_d[b - 1, :, 2 * i:2 * i + 2], y_out[:, 2 * i:2 * i + 2, :]).then_inc(turned, 16)

            run_steps(sp, step)
            sp.wait_ge(turned, 16 * 3 * B)

        @block.tensor
        def _(pe):
            def transposes(bank, src, c):
                for s in range(TC):
                    mm = nc.tensor.transpose(ps_m[bank][:, s * P:(s + 1) * P], src[:, s, c * P:(c + 1) * P],
                                             ident[:, :])
                return mm

            def warm_up(count):
                for _ in range(count):
                    nc.tensor.matmul(ps_o[:, 0:P], ident[:, :], ident[:, :], start=True, stop=True)

            def product(ps_out, left, right):
                for c in range(HC):
                    for n, (l, r) in enumerate(PASSES):
                        mm = nc.tensor.matmul(ps_out, left(l, c), right(r, c), start=c == 0 and n == 0,
                                              stop=c == HC - 1 and n == len(PASSES) - 1)
                return mm

            def job(b, n):
                _, kind, i, bank, off = jobs_of(b)[n]
                m = b + off
                if isinstance(b, int) and b == B and (kind, i) in WARM_JOBS:
                    pe.wait_ge(o_taken, B * GROUPS)
                    warm_up(WARM_JOBS[kind, i])
                user = last_user(b, n)
                if user is not None:
                    (_, k2, i2, _, off2), back = user
                    pe.wait_ge(taken[k2], nth(b + back + off2, PER[k2], i2))
                ps = ps_m[bank]
                if isinstance(m, int) and m == 0 and kind in READY_WEIGHTS:
                    pe.wait_ge(weight_lo, READY_WEIGHTS[kind])
                if kind == "nt":
                    if i == 0:
                        pe.wait_ge(ln1_done, nth(m, 1))
                    mm = transposes(bank, xn, i)
                elif kind == "qk":
                    w, half = (wq, wk)[i % 2], i // 2
                    if i == 0:
                        pe.wait_ge(taken["nt"], nth(m, 2, 1))
                    mm = product(ps[:, :], lambda a, c: w[:, a, c, half * P:(half + 1) * P],
                                 lambda a, c: xn_t[:, a, c, :])
                elif kind == "v":
                    for s in range(2):
                        t = 2 * i + s
                        mm = product(ps[:, s * H:(s + 1) * H], lambda a, c: xn_t[:, a, c, t * P:(t + 1) * P],
                                     lambda a, c: wv[:, a, c, :])
                elif kind == "y":
                    if i == 0:
                        pe.wait_ge(att_lo, nth(m, 2, 1))
                    for s in range(2):
                        t = 2 * i + s
                        mm = product(ps[:, s * H:(s + 1) * H], lambda a, c: att_t[:, a, c, t * P:(t + 1) * P],
                                     lambda a, c: wo[:, a, c, :])
                elif kind == "xt":
                    if i == 0:
                        pe.wait_ge(ln2_done, nth(m, 1))
                    mm = transposes(bank, xn2, i)
                elif kind == "sc":
                    pe.wait_ge(scored, nth(m, 1))
                    for t in range(TC):
                        mm = nc.tensor.transpose(ps[:, t * P:(t + 1) * P],
                                                 score[:, t:t + 1].broadcast_to([P, P]), ident[:, :])
                elif kind == "h":
                    if i == 0:
                        pe.wait_ge(taken["xt"], nth(m, 2, 1))
                    for s in range(2):
                        t = 2 * i + s
                        mm = product(ps[:, s * H:(s + 1) * H], lambda a, c: xn2_t[:, a, c, t * P:(t + 1) * P],
                                     lambda a, c: wb[:, a, c, :])
                mm.then_inc(ready[kind], 1)

            def scores(b, n):
                g, kc, pair = n // 8, n // 2 % TC, 2 * (n // 8) + n % 2
                if n % (UNITS // GROUPS) == 0:
                    pe.wait_ge(stacked[g], (b + 1) * STACKED)
                if not (isinstance(b, int) and b == 0 and n < 2):
                    pe.wait_ge(sigmoid_done, b * UNITS + n - 1)
                for tile in range(2):
                    rows = slice(tile * TILE, tile * TILE + SLOTS * D)
                    mm = nc.tensor.matmul(ps_s[:, n % 2, tile * S:(tile + 1) * S],
                                          k_st[rows, pair, kc * P:(kc + 1) * P], q_st[rows, pair, :],
                                          start=True, stop=True)
                mm.then_inc(scores_done, 1)

            def weighted_sum(b, r, kk, scores_run):
                g, p = r // 2, r % 2
                kc = 2 * p + kk
                if not scores_run:
                    pe.wait_ge(sigmoid_done, b * UNITS + 4 * r + 2 * kk + 2)
                if kk == 0:
                    if p == 0:
                        if g == 0:
                            pe.wait_ge(taken["v"], nth(b, 2, 1))
                        if g == GROUPS // 2:
                            pe.wait_ge(v_set, nth(b, 1))
                        if not (isinstance(b, int) and b == 0 and g == 0):
                            pe.wait_ge(o_taken, b * GROUPS + g)
                for j in range(GROUP):
                    mm = nc.tensor.matmul(ps_o[j * VW:(j + 1) * VW, :], v_x[:, kc, GROUP * g + j, :],
                                          pr[:, p, kk, j, :], start=kc == 0, stop=kc == TC - 1)
                mm.then_inc(av_done, 1)

            def step(b, on):
                for n in range(UNITS):
                    if on[0]:
                        if isinstance(b, int) and b == 0 and n == 0:
                            warm_up(WARM_SCORES)
                        scores(b, n)
                        if isinstance(b, int) and b == 0 and n < GROUP:
                            warm_up(WARM_UNIT)
                    if n % 2 == 1:
                        r, kk = n // 4 - 1, n % 4 // 2
                        if r < 0 and on[-1]:
                            weighted_sum(b - 1, r + 2 * GROUPS, kk, on[0])
                        if r >= 0 and on[0]:
                            weighted_sum(b, r, kk, True)
                    for m, (after, *_) in enumerate(jobs_of(b)):
                        if after == n:
                            job(b, m)

            pe.wait_ge(consts, 1)
            warm_up(WARM_START)
            run_steps(pe, step)

        @block.scalar
        def _(act):
            def hi_part(kind, b, i, dst):
                act.wait_ge(ready[kind], nth(b, PER[kind], i))
                nc.scalar.copy(dst[:, 0, i, :], ps_m[BANK[kind, i]][:, :]).then_inc(hi[kind], 1)

            def take_scores(b):
                act.wait_ge(ready["sc"], nth(b, 1))
                nc.scalar.copy(s_row[:, :], ps_m[BANK["sc", 0]][:, :]).then_inc(taken["sc"], 1)

            def first_part(b, i):
                act.wait_ge(ready["qk"], nth(b, 4, i))
                if not (isinstance(b, int) and b == 0):
                    act.wait_ge(spilled[i // 2], b * 32 + 32)
                nc.scalar.copy(split_part(i, 0), ps_m[BANK["qk", i]][:, :]).then_inc(part1, 1)

            def take_o(b, g):
                act.wait_ge(av_done, nth(b, 4 * GROUPS, 4 * g + 3))
                if not (isinstance(b, int) and b == 0 and g < 2):
                    act.wait_ge(o_turned, b * GROUPS + g - 1)
                nc.scalar.copy(o_t[:, g % 2, :], ps_o[:, :]).then_inc(o_taken, 1)

            def hi_attention(b, i):
                act.wait_ge(att_turned, nth(b, 2, i))
                if not (isinstance(b, int) and b == 0):
                    act.wait_ge(ready["y"], b * 2)
                nc.scalar.copy(att_t[:, 0, i, :], att[:, i, :]).then_inc(att_hi, 1)

            def sigmoid(b, n):
                r, kk, pair = n // 4, n // 2 % 2, n % 2
                act.wait_ge(scores_done, b * UNITS + n + 1)
                if n % 4 == 0 and not (isinstance(b, int) and b == 0 and r < 2):
                    act.wait_ge(av_done, b * 4 * GROUPS + 2 * (r - 1))
                nc.scalar.activation(pr[:, r % 2, kk, 2 * pair:2 * pair + 2, :].rearrange("p j q -> p (j q)"),
                                     ps_s[:, n % 2, :], ACT.Sigmoid, scale=SCALE).then_inc(sigmoid_done, 1)

            def square(b, i):
                act.wait_ge(ready["h"], nth(b, 2, i))
                nc.scalar.activation(gate_in[:, i, :], ps_m[BANK["h", i]][:, :], ACT.Square).then_inc(square_done, 1)

            def gate(b, i):
                act.wait_ge(arg_done, nth(b, 2, i))
                nc.scalar.activation(h_sig[:, i, :], gate_in[:, i, :], ACT.Sigmoid,
                                     scale=GELU_G * GELU_A).then_inc(gate_done, 1)

            def step(b, on):
                for n in range(UNITS + 1):
                    if on[0] and n < UNITS:
                        sigmoid(b, n)
                        if n in TAKE_O and n > TAKE_O[3]:
                            take_o(b, TAKE_O.index(n))
                    if on[-1] and n == TAKE_O[3]:
                        take_o(b - 1, 3)
                    if on[-1] and n == HI_1:
                        hi_attention(b - 1, 1)
                    if on[0] and n == HI_0:
                        hi_attention(b, 0)
                    for after, kind, i, _, off in jobs_of(b):
                        if after == n - GATE_LAG and kind == "h":
                            gate(b + off, i)
                        if after != n - 1:
                            continue
                        if kind == "qk":
                            first_part(b + off, i)
                        elif kind == "nt":
                            hi_part(kind, b + off, i, xn_t)
                        elif kind == "xt":
                            hi_part(kind, b + off, i, xn2_t)
                        elif kind == "sc":
                            take_scores(b + off)
                        elif kind == "h":
                            square(b + off, i)

            for i, (w, _) in enumerate(WEIGHTS):
                act.wait_ge(weight_in[i], 16)
                nc.scalar.copy(w[:, 0, :, :], raw[i]).then_inc(weight_hi, 1)
            run_steps(act, step)

        @block.vector
        def _(dve):
            def chunk_stats(src, stats, chunks):
                for s in chunks:
                    op = nc.vector.bn_stats(stats[:, s, :], src[:, s, :])
                return op

            def row_stats(b, stats, mv, mean, ve, stats_done):
                dve.wait_ge(stats_done, nth(b, 4, 0))
                m0, s0, m1, s1 = (stats[:, :, k] for k in (1, 2, 4, 5))
                nc.vector.tensor_tensor(mv[:, :, 0], m0, m1, ALU.add)
                nc.vector.tensor_tensor(mv[:, :, 1], m0, m1, ALU.subtract)
                nc.vector.tensor_tensor(mv[:, :, 2], s0, s1, ALU.add).then_inc(stats_done, 1)
                dve.wait_ge(stats_done, nth(b, 4, 1))
                nc.vector.tensor_scalar(mean[:, :], mv[:, :, 0], 0.5, None, ALU.mult)
                nc.vector.tensor_scalar(mv[:, :, 3], mv[:, :, 2], 1.0 / H, EPS_LN, ALU.mult, ALU.add)
                nc.vector.scalar_tensor_tensor(mv[:, :, 4], mv[:, :, 1], 0.25, mv[:, :, 1],
                                               ALU.mult, ALU.mult).then_inc(stats_done, 1)
                dve.wait_ge(stats_done, nth(b, 4, 2))
                nc.vector.tensor_tensor(ve[:, :], mv[:, :, 3], mv[:, :, 4], ALU.add).then_inc(stats_done, 1)

            def row_norm(b, src, mean, rstd, rstd_done, dst, done):
                dve.wait_ge(rstd_done, nth(b, 1))
                for s in range(TC):
                    op = nc.vector.tensor_scalar(dst[:, s, :], src[:, s, :], mean[:, s:s + 1], rstd[:, s:s + 1],
                                                 ALU.subtract, ALU.mult)
                op.then_inc(done, 1)

            def stats_1(b):
                if isinstance(b, int) and b == 0:
                    dve.wait_ge(x_first, 16)
                    chunk_stats(x_in, stats1, (0, 1))
                    dve.wait_ge(x_loaded, 16)
                    chunk_stats(x_in, stats1, (2, 3)).then_inc(stats1_done, 1)
                else:
                    dve.wait_ge(x_loaded, 16 * b + 16)
                    chunk_stats(x_in, stats1, range(TC)).then_inc(stats1_done, 1)
                row_stats(b, stats1, mv1, mean1, ve1, stats1_done)

            def norm_1(b, first):
                if not first:
                    dve.wait_ge(ready["nt"], nth(b - 1, 2, 1))
                row_norm(b, x_in, mean1, rstd1, rstd1_done, xn, ln1_done)

            def stats_2(b):
                for i in range(2):
                    residual(b, i)
                    dve.wait_ge(taken["y"], nth(b, 2, i))
                    op = chunk_stats(x1, stats2, (2 * i, 2 * i + 1))
                op.then_inc(stats2_done, 1)
                row_stats(b, stats2, mv2, mean2, ve2, stats2_done)

            def norm_2(b):
                row_norm(b, x1, mean2, rstd2, rstd2_done, xn2, ln2_done)

            def router(b):
                dve.wait_ge(ln2_done, nth(b, 1))
                for t in range(TC):
                    op = nc.vector.tensor_tensor_reduce(product[:, t, :], xn2[:, t, :], wr[:, :], 1.0, 0.0,
                                                        ALU.mult, ALU.add, score[:, t:t + 1])
                op.then_inc(scored, 1)

            def lo_part(kind, b, i, dst):
                dve.wait_ge(hi[kind], nth(b, 2, i))
                nc.vector.tensor_tensor(dst[:, 1, i, :], ps_m[BANK[kind, i]][:, :], dst[:, 0, i, :].bitcast(F32),
                                        ALU.subtract).then_inc(taken[kind], 1)

            def split_rest(b, i):
                dve.wait_ge(part1, nth(b, 4, i))
                nc.vector.tensor_tensor(split_part(i, 1), ps_m[BANK["qk", i]][:, :], split_part(i, 0).bitcast(F32),
                                        ALU.subtract).then_inc(taken["qk"], 1)

            def normalise(b, g):
                dve.wait_ge(o_taken, nth(b, GROUPS, g))
                if not (isinstance(b, int) and b == 0 and g == 0):
                    dve.wait_ge(att_set, b * GROUPS + g)
                    if g % 2 == 0:
                        dve.wait_ge(att_turned, b * 2 + g // 2)
                nc.vector.transpose(o_x[:, :, :].rearrange("p c w -> p (c w)"), o_t[:, g % 2, :]).then_inc(o_turned, 1)
                dve.wait_ge(o_turned, nth(b, GROUPS, g))
                nc.vector.tensor_scalar(den[:, g, :], o_x[:, :, D], EPS_W, None, ALU.add).then_inc(den_done, 1)
                dve.wait_ge(den_done, nth(b, 2 * GROUPS, 2 * g))
                nc.vector.reciprocal(rden[:, g, :], den[:, g, :]).then_inc(den_done, 1)
                dve.wait_ge(den_done, nth(b, 2 * GROUPS, 2 * g + 1))
                nc.vector.tensor_tensor(att_x[:, :, g % 2, :], o_x[:, :, 0:D],
                                        rden[:, g, :].unsqueeze(2).broadcast_to([P, BLOCKS, D]),
                                        ALU.mult).then_inc(att_set, 1)
                if g % 2 == 1:
                    dve.wait_ge(att_set, nth(b, GROUPS, g))
                    if not (isinstance(b, int) and b == 0):
                        dve.wait_ge(att_lo, nth(b - 1, 2, g // 2))
                    nc.vector.transpose(att[:, g // 2, :], att_x[:, :, :, :].rearrange("p c g d -> p (c g d)")
                                        ).then_inc(att_turned, 1)

            def take_values(b, i):
                dve.wait_ge(ready["v"], nth(b, 2, i))
                view = ps_m[BANK["v", i]][:, :].rearrange("p (t h) -> p t h", t=2)
                if i == 0 and not (isinstance(b, int) and b == 0):
                    dve.wait_ge(av_done, (b - 1) * 4 * GROUPS + 2 * GROUPS)
                nc.vector.tensor_copy(v_x[:, 2 * i:2 * i + 2, 0:HALF, 0:D],
                                      view[:, :, 0:P].rearrange("p t (h d) -> p t h d", d=D))
                nc.vector.tensor_copy(v_in[:, 2 * i:2 * i + 2, :], view[:, :, P:H]).then_inc(taken["v"], 1)

            def set_values(b):
                dve.wait_ge(taken["v"], nth(b, 2, 1))
                if not (isinstance(b, int) and b == 0):
                    dve.wait_ge(av_done, b * 4 * GROUPS)
                nc.vector.tensor_copy(v_x[:, :, HALF:HEADS, 0:D],
                                      v_in[:, :, :].rearrange("p t (h d) -> p t h d", d=D)).then_inc(v_set, 1)

            def residual(b, i):
                dve.wait_ge(ready["y"], nth(b, 2, i))
                dve.wait_ge(turned, 48 * b + 16)
                nc.vector.tensor_tensor(x1[:, 2 * i:2 * i + 2, :],
                                        ps_m[BANK["y", i]][:, :].rearrange("p (t h) -> p t h", t=2),
                                        x1[:, 2 * i:2 * i + 2, :], ALU.add).then_inc(taken["y"], 1)

            def count_higher(b, i):
                dve.wait_ge(taken["sc"], nth(b, 1))
                for t in (2 * i, 2 * i + 1):
                    own = score[:, t:t + 1]
                    if t > 0:
                        nc.vector.tensor_scalar(higher[:, t, 0:t * P], s_row[:, 0:t * P], own, None, ALU.is_ge,
                                                ALU.add, accum_out=count[:, t, 0:1])
                    nc.vector.tensor_scalar(higher[:, t, t * P:S], s_row[:, t * P:S], own, None, ALU.is_gt, ALU.add,
                                            accum_out=count[:, t, 1:2])
                    op = nc.vector.scalar_tensor_tensor(higher[:, t, S:S + P], s_row[:, t * P:(t + 1) * P], own,
                                                        before[:, :], ALU.is_equal, ALU.mult,
                                                        accum_out=count[:, t, 2:3])
                if i == 1:
                    op.then_inc(rank_done, 1)

            def choose(b):
                dve.wait_ge(rank_done, nth(b, 4, 0))
                nc.vector.tensor_reduce(rank[:, :], count[:, :, :], AX_X, ALU.add).then_inc(rank_done, 1)
                dve.wait_ge(rank_done, nth(b, 4, 1))
                nc.vector.tensor_scalar(routed[:, :], rank[:, :], float(TOP), None, ALU.is_lt).then_inc(rank_done, 1)
                nc.vector.tensor_scalar(passed[:, :], rank[:, :], float(TOP), None, ALU.is_ge).then_inc(rank_done, 1)

            def residual_base(b, i):
                dve.wait_ge(rank_done, nth(b, 4, 3))
                for t in (2 * i, 2 * i + 1):
                    op = nc.vector.scalar_tensor_tensor(base[:, t, :], xn2[:, t, :], passed[:, t:t + 1], x1[:, t, :],
                                                        ALU.mult, ALU.add)
                op.then_inc(base_done, 1)

            def gelu_arg(b, i):
                dve.wait_ge(square_done, nth(b, 2, i))
                nc.vector.scalar_tensor_tensor(gate_in[:, i, :], gate_in[:, i, :], 1.0 / GELU_A,
                                               ps_m[BANK["h", i]][:, :], ALU.add, ALU.mult).then_inc(arg_done, 1)

            def gelu(b, i):
                dve.wait_ge(gate_done, nth(b, 2, i))
                dve.wait_ge(rank_done, nth(b, 4, 3))
                for s in range(2):
                    t = 2 * i + s
                    op = nc.vector.scalar_tensor_tensor(h_out[:, t, :], h_sig[:, i, s * H:(s + 1) * H],
                                                        routed[:, t:t + 1],
                                                        ps_m[BANK["h", i]][:, s * H:(s + 1) * H],
                                                        ALU.mult, ALU.mult)
                op.then_inc(taken["h"], 1)
                if isinstance(b, int) and b == B - 1 and i == 1:
                    dve.wait_ge(base_done, nth(b, 2, 1))
                    dve.wait_ge(taken["h"], nth(b, 2, 1))
                    dve.wait_ge(turned, 48 * b + 16)
                    nc.vector.tensor_tensor(y_out[:, 2:4, :], base[:, 2:4, :], h_out[:, 2:4, :],
                                            ALU.add).then_inc(last_ready, 1)

            def step(b, on):
                if on[1] and not (isinstance(b, int) and b == -1):
                    stats_1(b + 1)
                if on[-1]:
                    normalise(b - 1, 3)
                if on[0] and not (isinstance(b, int) and b == 0):
                    split_rest(b, 2)
                    split_rest(b, 3)
                if on[0]:
                    set_values(b)
                if on[1] and not (isinstance(b, int) and b == -1):
                    norm_1(b + 1, False)
                if on[-1]:
                    stats_2(b - 1)
                if on[0]:
                    normalise(b, 0)
                if on[-1]:
                    norm_2(b - 1)
                if on[1] and not (isinstance(b, int) and b == -1):
                    lo_part("nt", b + 1, 0, xn_t)
                    lo_part("nt", b + 1, 1, xn_t)
                if on[-1]:
                    router(b - 1)
                    lo_part("xt", b - 1, 0, xn2_t)
                    lo_part("xt", b - 1, 1, xn2_t)
                    count_higher(b - 1, 0)
                if on[1]:
                    split_rest(b + 1, 0)
                if on[-1]:
                    gelu_arg(b - 1, 0)
                    count_higher(b - 1, 1)
                    choose(b - 1)
                    gelu(b - 1, 0)
                    gelu_arg(b - 1, 1)
                if on[1]:
                    split_rest(b + 1, 1)
                if on[0]:
                    normalise(b, 1)
                if on[-1]:
                    residual_base(b - 1, 0)
                    residual_base(b - 1, 1)
                if on[1]:
                    take_values(b + 1, 0)
                if on[-1]:
                    gelu(b - 1, 1)
                if on[0]:
                    normalise(b, 2)
                if on[1]:
                    take_values(b + 1, 1)
                if isinstance(b, int) and b == -1:
                    split_rest(0, 2)
                    split_rest(0, 3)

            stats_1(0)
            for i, (w, _) in enumerate(WEIGHTS):
                if i == 1:
                    norm_1(0, True)
                if i == 3:
                    lo_part("nt", 0, 0, xn_t)
                    lo_part("nt", 0, 1, xn_t)
                dve.wait_ge(weight_hi, i + 1)
                nc.vector.tensor_tensor(w[:, 1, :, :], raw[i], w[:, 0, :, :].bitcast(F32),
                                        ALU.subtract).then_inc(weight_lo, 1)
            dve.wait_ge(consts, 1)
            dve.wait_ge(wr_in, 16)
            run_steps(dve, step)

        @block.gpsimd
        def _(pool):
            nc.gpsimd.memset(ident[:, :], 0.0)
            nc.gpsimd.memset(before[:, :], 0.0)
            nc.gpsimd.memset(minus_half[:, :], -0.5)
            nc.gpsimd.memset(count[:, :, :], 0.0)
            nc.gpsimd.memset(v_x[:, :, :, :], 1.0).then_inc(zeros_set, 1)
            pool.wait_ge(zeros_set, 1)
            nc.gpsimd.affine_select(out=ident[:, :], in_=ident[:, :], compare_op=ALU.not_equal, fill=1.0,
                                    base=0, pattern=[[-1, P]], channel_multiplier=1)
            nc.gpsimd.affine_select(out=before[:, :], in_=before[:, :], compare_op=ALU.is_ge, fill=1.0,
                                    base=0, pattern=[[1, P]], channel_multiplier=-1).then_inc(consts, 1)

            def inverse_root(b, ve, rstd, stats_done, rstd_done):
                pool.wait_ge(stats_done, nth(b, 4, 3))
                nc.gpsimd.tensor_tensor(rstd[:, :], ve[:, :], minus_half[:, :], ALU.pow).then_inc(rstd_done, 1)

            def lo_attention(b, i):
                pool.wait_ge(att_hi, nth(b, 2, i))
                nc.gpsimd.tensor_tensor(att_t[:, 1, i, :], att[:, i, :], att_t[:, 0, i, :].bitcast(F32),
                                        ALU.subtract).then_inc(att_lo, 1)

            def output(b, i):
                if isinstance(b, int) and b == B - 1 and i == 1:
                    return
                pool.wait_ge(base_done, nth(b, 2, i))
                pool.wait_ge(turned, 48 * b + 16)
                pool.wait_ge(taken["h"], nth(b, 2, i))
                chunks = slice(2 * i, 2 * i + 2)
                nc.gpsimd.tensor_tensor(y_out[:, chunks, :], base[:, chunks, :], h_out[:, chunks, :],
                                        ALU.add).then_inc(out_ready, 1)

            def step(b, on):
                if on[1]:
                    inverse_root(b + 1, ve1, rstd1, stats1_done, rstd1_done)
                if on[-1]:
                    lo_attention(b - 1, 1)
                    inverse_root(b - 1, ve2, rstd2, stats2_done, rstd2_done)
                    output(b - 1, 0)
                if on[0]:
                    lo_attention(b, 0)
                if on[-1]:
                    output(b - 1, 1)

            run_steps(pool, step)


def kernel(**inputs):
    import numpy as _np
    import concourse.bacc as _bacc
    from concourse import mybir as _mybir
    from concourse.bass_utils import run_bass_kernel_spmd as _run

    nc = _bacc.Bacc("TRN2", target_bir_lowering=False, num_devices=1)
    arrays, args = {}, []
    for name in ("L0_attn_x", "L0_attn_Wq", "L0_attn_Wk", "L0_attn_Wv", "L0_attn_Wo",
                 "L0_ffn_w_router", "L0_ffn_w_block"):
        a = _np.asarray(inputs[name])
        if name.startswith("L0_attn_W"):
            a = a.T
        if name in ("L0_attn_Wq", "L0_attn_Wk"):
            a = a.reshape(H, 2, HALF // 2, 2, D).transpose(0, 1, 4, 3, 2).reshape(H, H)
        if name == "L0_attn_Wo":
            a = a.reshape(2, 2, GROUP, D, H).transpose(0, 2, 1, 3, 4).reshape(H, H)
        a = _np.ascontiguousarray(a)
        arrays[f"in_{name}"] = a
        args.append(nc.dram_tensor(f"in_{name}", a.shape, _mybir.dt.from_np(a.dtype), kind="ExternalInput").ap())
    args.append(nc.dram_tensor("out_0", (B, S, H), F32, kind="ExternalOutput").ap())
    layer(nc, *args)
    r = _run(nc, [arrays], core_ids=[0])
    return r.results[0]["out_0"]
```
